# Optimizing a Trainium2 kernel written in Bass

```python
import numpy as np
import jax
import jax.numpy as jnp

def _softmax(x, axis=-1):
    return jax.nn.softmax(x, axis=axis)

def _gelu(x):
    return jax.nn.gelu(x, approximate=True)

def _silu(x):
    return jax.nn.silu(x)

def _sigmoid(x):
    return jax.nn.sigmoid(x)

def _layernorm(x, axis=-1, eps=1e-05):
    m = jnp.mean(x, axis=axis, keepdims=True)
    v = jnp.var(x, axis=axis, keepdims=True)
    return (x - m) / jnp.sqrt(v + eps)

def _scatter_add(tgt, idx, src, axis=0):
    return tgt.at[idx].add(src)

def _segment_sum(src, seg, n):
    return jax.ops.segment_sum(src, seg, n)
kernel_name = 'mk_dlrm_tower_d1_rec_r8_dd8236'

def setup_inputs(seed: int=0):
    np.random.seed(seed)
    _w = jnp.asarray

    def _rec_inputs():
        import jax
        import jax.numpy as jnp
        _tk = jax.random.key(seed)
        dense_ctx = jax.random.normal(jax.random.fold_in(_tk, 190), (512, 16), jnp.float32)
        ids = jnp.stack([jax.random.randint(jax.random.fold_in(_tk, 200 + f), (512,), 0, v, jnp.int32) for f, v in enumerate([1250, 1000, 1250, 1000, 12500, 1000, 1250, 1250, 1000, 125000, 1250, 125000, 1250, 1000, 1000, 125000, 12500, 125000, 1000, 12500, 125000, 125000, 125000, 12500, 1250, 125000, 1250, 12500, 125000, 125000, 1250, 12500, 12500, 1250, 1250, 1000, 1250, 1250, 12500])], axis=1)
        tbl_0 = 0.05 * jax.random.normal(jax.random.fold_in(_tk, 500 + 0), (1250, 16), jnp.float32)
        tbl_1 = 0.05 * jax.random.normal(jax.random.fold_in(_tk, 500 + 1), (1000, 16), jnp.float32)
        tbl_2 = 0.05 * jax.random.normal(jax.random.fold_in(_tk, 500 + 2), (1250, 16), jnp.float32)
        tbl_3 = 0.05 * jax.random.normal(jax.random.fold_in(_tk, 500 + 3), (1000, 16), jnp.float32)
        tbl_4 = 0.05 * jax.random.normal(jax.random.fold_in(_tk, 500 + 4), (12500, 16), jnp.float32)
        tbl_5 = 0.05 * jax.random.normal(jax.random.fold_in(_tk, 500 + 5), (1000, 16), jnp.float32)
        tbl_6 = 0.05 * jax.random.normal(jax.random.fold_in(_tk, 500 + 6), (1250, 16), jnp.float32)
        tbl_7 = 0.05 * jax.random.normal(jax.random.fold_in(_tk, 500 + 7), (1250, 16), jnp.float32)
        tbl_8 = 0.05 * jax.random.normal(jax.random.fold_in(_tk, 500 + 8), (1000, 16), jnp.float32)
        tbl_9 = 0.05 * jax.random.normal(jax.random.fold_in(_tk, 500 + 9), (125000, 16), jnp.float32)
        tbl_10 = 0.05 * jax.random.normal(jax.random.fold_in(_tk, 500 + 10), (1250, 16), jnp.float32)
        tbl_11 = 0.05 * jax.random.normal(jax.random.fold_in(_tk, 500 + 11), (125000, 16), jnp.float32)
        tbl_12 = 0.05 * jax.random.normal(jax.random.fold_in(_tk, 500 + 12), (1250, 16), jnp.float32)
        tbl_13 = 0.05 * jax.random.normal(jax.random.fold_in(_tk, 500 + 13), (1000, 16), jnp.float32)
        tbl_14 = 0.05 * jax.random.normal(jax.random.fold_in(_tk, 500 + 14), (1000, 16), jnp.float32)
        tbl_15 = 0.05 * jax.random.normal(jax.random.fold_in(_tk, 500 + 15), (125000, 16), jnp.float32)
        tbl_16 = 0.05 * jax.random.normal(jax.random.fold_in(_tk, 500 + 16), (12500, 16), jnp.float32)
        tbl_17 = 0.05 * jax.random.normal(jax.random.fold_in(_tk, 500 + 17), (125000, 16), jnp.float32)
        tbl_18 = 0.05 * jax.random.normal(jax.random.fold_in(_tk, 500 + 18), (1000, 16), jnp.float32)
        tbl_19 = 0.05 * jax.random.normal(jax.random.fold_in(_tk, 500 + 19), (12500, 16), jnp.float32)
        tbl_20 = 0.05 * jax.random.normal(jax.random.fold_in(_tk, 500 + 20), (125000, 16), jnp.float32)
        tbl_21 = 0.05 * jax.random.normal(jax.random.fold_in(_tk, 500 + 21), (125000, 16), jnp.float32)
        tbl_22 = 0.05 * jax.random.normal(jax.random.fold_in(_tk, 500 + 22), (125000, 16), jnp.float32)
        tbl_23 = 0.05 * jax.random.normal(jax.random.fold_in(_tk, 500 + 23), (12500, 16), jnp.float32)
        tbl_24 = 0.05 * jax.random.normal(jax.random.fold_in(_tk, 500 + 24), (1250, 16), jnp.float32)
        tbl_25 = 0.05 * jax.random.normal(jax.random.fold_in(_tk, 500 + 25), (125000, 16), jnp.float32)
        tbl_26 = 0.05 * jax.random.normal(jax.random.fold_in(_tk, 500 + 26), (1250, 16), jnp.float32)
        tbl_27 = 0.05 * jax.random.normal(jax.random.fold_in(_tk, 500 + 27), (12500, 16), jnp.float32)
        tbl_28 = 0.05 * jax.random.normal(jax.random.fold_in(_tk, 500 + 28), (125000, 16), jnp.float32)
        tbl_29 = 0.05 * jax.random.normal(jax.random.fold_in(_tk, 500 + 29), (125000, 16), jnp.float32)
        tbl_30 = 0.05 * jax.random.normal(jax.random.fold_in(_tk, 500 + 30), (1250, 16), jnp.float32)
        tbl_31 = 0.05 * jax.random.normal(jax.random.fold_in(_tk, 500 + 31), (12500, 16), jnp.float32)
        tbl_32 = 0.05 * jax.random.normal(jax.random.fold_in(_tk, 500 + 32), (12500, 16), jnp.float32)
        tbl_33 = 0.05 * jax.random.normal(jax.random.fold_in(_tk, 500 + 33), (1250, 16), jnp.float32)
        tbl_34 = 0.05 * jax.random.normal(jax.random.fold_in(_tk, 500 + 34), (1250, 16), jnp.float32)
        tbl_35 = 0.05 * jax.random.normal(jax.random.fold_in(_tk, 500 + 35), (1000, 16), jnp.float32)
        tbl_36 = 0.05 * jax.random.normal(jax.random.fold_in(_tk, 500 + 36), (1250, 16), jnp.float32)
        tbl_37 = 0.05 * jax.random.normal(jax.random.fold_in(_tk, 500 + 37), (1250, 16), jnp.float32)
        tbl_38 = 0.05 * jax.random.normal(jax.random.fold_in(_tk, 500 + 38), (12500, 16), jnp.float32)
        _rk = jax.random.fold_in(_tk, 7)
        W_top1 = 0.0606339 * jax.random.normal(jax.random.fold_in(_tk, 801), (272, 512), jnp.float32)
        W_top2 = 0.0441942 * jax.random.normal(jax.random.fold_in(_tk, 802), (512, 256), jnp.float32)
        W_top3 = 0.0625 * jax.random.normal(jax.random.fold_in(_tk, 803), (256, 1), jnp.float32)
        b_top1 = jnp.zeros((512,), jnp.float32)
        b_top2 = jnp.zeros((256,), jnp.float32)
        return (dense_ctx, ids, tbl_0, tbl_1, tbl_2, tbl_3, tbl_4, tbl_5, tbl_6, tbl_7, tbl_8, tbl_9, tbl_10, tbl_11, tbl_12, tbl_13, tbl_14, tbl_15, tbl_16, tbl_17, tbl_18, tbl_19, tbl_20, tbl_21, tbl_22, tbl_23, tbl_24, tbl_25, tbl_26, tbl_27, tbl_28, tbl_29, tbl_30, tbl_31, tbl_32, tbl_33, tbl_34, tbl_35, tbl_36, tbl_37, tbl_38, W_top1, b_top1, W_top2, b_top2, W_top3)
    dense_ctx, ids, tbl_0, tbl_1, tbl_2, tbl_3, tbl_4, tbl_5, tbl_6, tbl_7, tbl_8, tbl_9, tbl_10, tbl_11, tbl_12, tbl_13, tbl_14, tbl_15, tbl_16, tbl_17, tbl_18, tbl_19, tbl_20, tbl_21, tbl_22, tbl_23, tbl_24, tbl_25, tbl_26, tbl_27, tbl_28, tbl_29, tbl_30, tbl_31, tbl_32, tbl_33, tbl_34, tbl_35, tbl_36, tbl_37, tbl_38, W_top1, b_top1, W_top2, b_top2, W_top3 = _rec_inputs()

    def _L0_rec_setup():
        import jax, jax.numpy as jnp
        import numpy as np
        B, F0, D = (256, 39, 16)
        LAYER_SIZES = [128, 128, 128]
        key = jax.random.key(seed)
        ks = jax.random.split(key, 1 + 2 * len(LAYER_SIZES))
        inputs = jax.random.normal(ks[0], (B, F0, D), dtype=jnp.float32)
        out = {'inputs': inputs}
        field_nums = [F0]
        for i, size in enumerate(LAYER_SIZES):
            fk = field_nums[-1]
            fan_in = F0 * fk
            scale = np.sqrt(2.0 / (fan_in + size)).astype(np.float32)
            out[f'w{i}'] = jax.random.normal(ks[1 + 2 * i], (F0, fk, size), dtype=jnp.float32) * scale
            out[f'b{i}'] = jnp.zeros((size,), dtype=jnp.float32)
            field_nums.append(size // 2)
        return out
    _L0_rec_all = _L0_rec_setup()
    _L0_rec_in = {k: v for k, v in _L0_rec_all.items() if k in ('w0', 'w1', 'w2', 'b0', 'b1', 'b2')}
    del _L0_rec_all
    return {'dense_ctx': dense_ctx, 'ids': ids, 'tbl_0': tbl_0, 'tbl_1': tbl_1, 'tbl_2': tbl_2, 'tbl_3': tbl_3, 'tbl_4': tbl_4, 'tbl_5': tbl_5, 'tbl_6': tbl_6, 'tbl_7': tbl_7, 'tbl_8': tbl_8, 'tbl_9': tbl_9, 'tbl_10': tbl_10, 'tbl_11': tbl_11, 'tbl_12': tbl_12, 'tbl_13': tbl_13, 'tbl_14': tbl_14, 'tbl_15': tbl_15, 'tbl_16': tbl_16, 'tbl_17': tbl_17, 'tbl_18': tbl_18, 'tbl_19': tbl_19, 'tbl_20': tbl_20, 'tbl_21': tbl_21, 'tbl_22': tbl_22, 'tbl_23': tbl_23, 'tbl_24': tbl_24, 'tbl_25': tbl_25, 'tbl_26': tbl_26, 'tbl_27': tbl_27, 'tbl_28': tbl_28, 'tbl_29': tbl_29, 'tbl_30': tbl_30, 'tbl_31': tbl_31, 'tbl_32': tbl_32, 'tbl_33': tbl_33, 'tbl_34': tbl_34, 'tbl_35': tbl_35, 'tbl_36': tbl_36, 'tbl_37': tbl_37, 'tbl_38': tbl_38, 'W_top1': W_top1, 'b_top1': b_top1, 'W_top2': W_top2, 'b_top2': b_top2, 'W_top3': W_top3, 'L0_rec_w0': _L0_rec_in['w0'], 'L0_rec_w1': _L0_rec_in['w1'], 'L0_rec_w2': _L0_rec_in['w2'], 'L0_rec_b0': _L0_rec_in['b0'], 'L0_rec_b1': _L0_rec_in['b1'], 'L0_rec_b2': _L0_rec_in['b2']}

def reference(dense_ctx, ids, tbl_0, tbl_1, tbl_2, tbl_3, tbl_4, tbl_5, tbl_6, tbl_7, tbl_8, tbl_9, tbl_10, tbl_11, tbl_12, tbl_13, tbl_14, tbl_15, tbl_16, tbl_17, tbl_18, tbl_19, tbl_20, tbl_21, tbl_22, tbl_23, tbl_24, tbl_25, tbl_26, tbl_27, tbl_28, tbl_29, tbl_30, tbl_31, tbl_32, tbl_33, tbl_34, tbl_35, tbl_36, tbl_37, tbl_38, W_top1, b_top1, W_top2, b_top2, W_top3, L0_rec_w0, L0_rec_w1, L0_rec_w2, L0_rec_b0, L0_rec_b1, L0_rec_b2):
    import jax
    import jax.numpy as jnp

    def _L0_rec_ref(inputs, w0, w1, w2, b0, b1, b2):
        import jax, jax.numpy as jnp
        import numpy as np
        B, F0, D = (256, 39, 16)
        LAYER_SIZES = [128, 128, 128]
        x0 = inputs
        xk = inputs
        params = [(w0, b0), (w1, b1), (w2, b2)]
        n_layers = len(params)
        direct = []
        for idx, (W, b) in enumerate(params):
            z = jnp.einsum('bhd,bkd,hks->bsd', x0, xk, W) + b[None, :, None]
            z = jax.nn.relu(z)
            if idx != n_layers - 1:
                half = z.shape[1] // 2
                xk = z[:, :half, :]
                direct.append(z[:, half:, :])
            else:
                direct.append(z)
        logit = jnp.sum(jnp.concatenate(direct, axis=1), axis=-1)
        return logit
    e = jnp.stack([tbl_0[ids[:, 0]], tbl_1[ids[:, 1]], tbl_2[ids[:, 2]], tbl_3[ids[:, 3]], tbl_4[ids[:, 4]], tbl_5[ids[:, 5]], tbl_6[ids[:, 6]], tbl_7[ids[:, 7]], tbl_8[ids[:, 8]], tbl_9[ids[:, 9]], tbl_10[ids[:, 10]], tbl_11[ids[:, 11]], tbl_12[ids[:, 12]], tbl_13[ids[:, 13]], tbl_14[ids[:, 14]], tbl_15[ids[:, 15]], tbl_16[ids[:, 16]], tbl_17[ids[:, 17]], tbl_18[ids[:, 18]], tbl_19[ids[:, 19]], tbl_20[ids[:, 20]], tbl_21[ids[:, 21]], tbl_22[ids[:, 22]], tbl_23[ids[:, 23]], tbl_24[ids[:, 24]], tbl_25[ids[:, 25]], tbl_26[ids[:, 26]], tbl_27[ids[:, 27]], tbl_28[ids[:, 28]], tbl_29[ids[:, 29]], tbl_30[ids[:, 30]], tbl_31[ids[:, 31]], tbl_32[ids[:, 32]], tbl_33[ids[:, 33]], tbl_34[ids[:, 34]], tbl_35[ids[:, 35]], tbl_36[ids[:, 36]], tbl_37[ids[:, 37]], tbl_38[ids[:, 38]]], axis=1)
    z = _L0_rec_ref(e, L0_rec_w0, L0_rec_w1, L0_rec_w2, L0_rec_b0, L0_rec_b1, L0_rec_b2)
    z = z.reshape(z.shape[0], -1)
    h = jnp.concatenate([z, dense_ctx], axis=1)
    h = jnp.maximum(h @ W_top1 + b_top1, 0.0)
    h = jnp.maximum(h @ W_top2 + b_top2, 0.0)
    y = h @ W_top3
    return y

_drawn_inputs = setup_inputs


def setup_inputs(seed=0):
    import zlib

    import numpy as np

    out = dict(_drawn_inputs(seed))
    spreads = {'b_top1': (0.0, 2.0),
     'b_top2': (0.0, 2.0),
     'L0_rec_b0': (0.0, 0.343),
     'L0_rec_b1': (0.0, 0.5),
     'L0_rec_b2': (0.0, 0.8)}
    factors = {'tbl_0': 8.0,
     'tbl_1': 8.0,
     'tbl_2': 8.0,
     'tbl_3': 8.0,
     'tbl_4': 8.0,
     'tbl_5': 8.0,
     'tbl_6': 8.0,
     'tbl_7': 8.0,
     'tbl_8': 8.0,
     'tbl_9': 8.0,
     'tbl_10': 8.0,
     'tbl_11': 8.0,
     'tbl_12': 8.0,
     'tbl_13': 8.0,
     'tbl_14': 8.0,
     'tbl_15': 8.0,
     'tbl_16': 8.0,
     'tbl_17': 8.0,
     'tbl_18': 8.0,
     'tbl_19': 8.0,
     'tbl_20': 8.0,
     'tbl_21': 8.0,
     'tbl_22': 8.0,
     'tbl_23': 8.0,
     'tbl_24': 8.0,
     'tbl_25': 8.0,
     'tbl_26': 8.0,
     'tbl_27': 8.0,
     'tbl_28': 8.0,
     'tbl_29': 8.0,
     'tbl_30': 8.0,
     'tbl_31': 8.0,
     'tbl_32': 8.0,
     'tbl_33': 8.0,
     'tbl_34': 8.0,
     'tbl_35': 8.0,
     'tbl_36': 8.0,
     'tbl_37': 8.0,
     'tbl_38': 8.0,
     'L0_rec_w0': 8.0,
     'L0_rec_w1': 6.084,
     'L0_rec_w2': 4.807,
     'dense_ctx': 8.0}
    for name, (base, spread) in spreads.items():
        noise = np.random.default_rng([zlib.crc32(name.encode()), seed]).standard_normal(out[name].shape)
        drawn = base * np.exp(spread * noise) if base else spread * noise
        out[name] = jnp.asarray(drawn.astype(out[name].dtype))
    for name, factor in factors.items():
        out[name] = (out[name] * factor).astype(out[name].dtype)
    return out
```

```python
from contextlib import ExitStack

import concourse.bass as bass
from concourse import mybir

F32 = mybir.dt.float32
F32R = mybir.dt.float32r
I32 = mybir.dt.int32
ALU = mybir.AluOpType
ACT = mybir.ActivationFunctionType
AX_X = mybir.AxisListType.X

P = 128
SPLIT = {0: (4,), 1: (4, 6, 9, 11, 14, 16, 18), 2: (4, 7, 9, 12, 14, 17, 19)}
P_RING, HALF_RING, B_RING = 4, 2, 3
LOW_LAG = 2


def cin_tower(nc, dense_ctx, ids, tables, W_top1, b_top1, W_top2, b_top2, W_top3, cin_w, cin_b, out):
    B, DENSE = dense_ctx.shape
    F = len(tables)
    D = tables[0].shape[1]
    S_OUT = cin_w[0].shape[2]
    MAPS = cin_w[1].shape[1]
    H1, H2 = W_top1.shape[1], W_top2.shape[1]

    BT = B // P
    BB = P // 2
    NB = B // BB
    COLS = BB * D
    BANK = 512
    CH = COLS // BANK

    SHIFTS = F // 2 + 1
    SH_PER = P // F
    TILES = {0: -(-SHIFTS // SH_PER), 1: -(-F * MAPS // P), 2: -(-F * MAPS // P)}
    ROWS = {0: [F * min(SH_PER, SHIFTS - SH_PER * t) for t in range(TILES[0])]}
    ROWS[1] = ROWS[2] = [min(P, F * MAPS - P * t) for t in range(TILES[1])]
    assert B % P == 0 and MAPS == 64 and S_OUT == P and F % 2 == 1 and D == 16

    def layer(l, db):
        return [(l, t, db) for t in range(TILES[l])]

    half = layer(0, 1) + layer(2, 0) + layer(1, 1)
    prologue = layer(0, 0) + layer(1, 0)
    body = half + half
    tail = half + layer(2, 1)
    PRO, BODY, HALF = len(prologue), len(body), len(half)

    def splits(jobs):
        return sum(t in SPLIT[l] for l, t, _ in jobs)

    PRO_S, BODY_S = splits(prologue), splits(body)
    assert BODY_S % HALF_RING == 0

    whole_of = {l: [t for t in range(TILES[l]) if t not in SPLIT[l]] for l in range(3)}
    w_at, n_whole, n_split = {}, 0, 0
    for l in range(3):
        for t in range(TILES[l]):
            if t in SPLIT[l]:
                w_at[l, t], n_split = n_split, n_split + 1
            else:
                w_at[l, t], n_whole = n_whole, n_whole + 1

    with ExitStack() as ctx:
        def sb(name, shape, dt=F32):
            return ctx.enter_context(nc.sbuf_tensor(name, shape, dt))

        def psum(name, shape):
            return ctx.enter_context(nc.psum_tensor(name, shape, F32))

        def sem(name):
            return ctx.enter_context(nc.semaphore(name))

        x0rep = sb("x0rep", [P, TILES[1], COLS])
        staged = x0rep[:].rearrange("p t c -> p (t c)")
        w_whole = sb("w_whole", [P, n_whole, S_OUT])
        w_high = sb("w_high", [P, n_split, S_OUT], F32R)
        w_low = sb("w_low", [P, n_split, S_OUT], F32R)
        prod = sb("prod", [P, P_RING, COLS])
        high = sb("high", [P, HALF_RING, COLS], F32R)
        low = sb("low", [P, HALF_RING, COLS], F32R)
        xk = {1: sb("xk1", [P, COLS]), 2: sb("xk2", [P, COLS])}
        x0a = sb("x0a", [P, COLS])
        x0b = sb("x0b", [P, B_RING, COLS])
        direct01 = sb("direct01", [P, COLS])
        direct2 = sb("direct2", [P, COLS])
        emb = sb("emb", [P, F, D])
        x0t = sb("x0t", [F, 2, D, BB])
        ids_sb = sb("ids_sb", [P, BT, F], I32)
        ident = sb("ident", [P, P])
        sums = sb("sums", [P, 2, B])
        dense_sb = sb("dense_sb", [P, BT, DENSE])
        dense_t = sb("dense_t", [DENSE, B])
        wt1 = sb("wt1", [P, 3, H1])
        wt2 = sb("wt2", [P, H1 // P, H2])
        wt3 = sb("wt3", [P, H2 // P])
        bias = sb("bias", [P, 3 + H1 // P + H2 // P])
        y_sb = sb("y_sb", [1, B])
        MAIN = B - BB
        mlp = x0b[:].rearrange("p r c -> p (r c)")
        h1 = mlp[:, 0:H1 // P * MAIN].rearrange("p (m n) -> p m n", n=MAIN)
        h2 = mlp[:, H1 // P * MAIN:(H1 + H2) // P * MAIN].rearrange("p (m n) -> p m n", n=MAIN)

        z = [psum(f"z{l}", [P, COLS]) for l in range(3)]
        spare = [psum(f"spare{i}", [P, BANK]) for i in range(2)]

        x0_dram = nc.dram_tensor("x0_dram", (NB, 2 * F, COLS), F32, kind="Internal").ap()

        s_ids = sem("ids_loaded")
        s_dense = sem("dense_loaded")
        s_wraw = sem("cin_weights_loaded")
        s_zero = sem("staging_zeroed")
        s_mlpw = sem("mlp_weights_loaded")
        s_bias = sem("biases_loaded")
        s_ident = sem("identity_made")
        s_wsum = sem("pair_weights_added")
        s_wcopy = sem("whole_weights_copied")
        s_whigh = sem("high_weights_made")
        s_wlow = sem("low_weights_made")
        s_gather = sem("rows_gathered")
        s_turned = sem("transposes_done")
        s_x0t = sem("x0t_copied")
        s_dram = sem("x0_written")
        s_x0a = sem("x0a_loaded")
        s_x0b = [sem(f"x0b{i}_loaded") for i in range(B_RING)]
        s_x0rep = [sem(f"x0rep{t}_loaded") for t in range(TILES[1])]
        s_prod = sem("products_done")
        s_high = sem("highs_done")
        s_low = sem("lows_done")
        s_tile = sem("tiles_contracted")
        s_xk = {1: sem("xk1_ready"), 2: sem("xk2_ready")}
        s_read = [sem(f"z{l}_evacuated") for l in range(3)]
        s_sum01 = sem("direct01_summed")
        s_sum2 = sem("direct2_summed")
        s_dense_turned = sem("dense_transposed")
        s_dense_copied = sem("dense_copied")
        s_mlp_mm = sem("mlp_matmuls_done")
        s_mlp_act = sem("mlp_activated")
        s_out = sem("out_written")

        def block_rows(b):
            if isinstance(b, int):
                return x0_dram[b]
            return x0_dram[bass.ds(b, 1), :, :].rearrange("o r c -> (o r) c")

        RAW = {1: 0, 2: TILES[1] * S_OUT, 0: 2 * TILES[1] * S_OUT}
        RAW_T = RAW[0] + TILES[0] * S_OUT

        def raw(l, t, rows):
            return staged[0:rows, RAW[l] + t * S_OUT:RAW[l] + (t + 1) * S_OUT]

        def walk(jobs):
            n = 0
            for pos, (l, t, db) in enumerate(jobs):
                split = t in SPLIT[l]
                yield pos, l, t, db, (n if split else None)
                n += split

        def run(kind, bt=None):
            if kind == "prologue":
                return prologue, 0, 0, 0, (BODY - PRO) % P_RING, (BODY_S - PRO_S) % HALF_RING
            jobs = body if kind == "body" else tail
            return jobs, PRO + bt * BODY, PRO_S + bt * BODY_S, bt * 2, 0, 0

        def block_of(pos, db, b0):
            return b0 + (pos // HALF) + db if pos < 2 * HALF else b0 + db

        def of_tail(kind, pos, db, b0):
            return b0 + db if kind == "tail" else block_of(pos, db, b0)

        def last_of(l, t):
            return t == TILES[l] - 1

        blk = ctx.enter_context(nc.Block())

        @blk.sync
        def _(sp):
            sp.dma_start(ids_sb[:], ids.rearrange("(t p) f -> p t f", p=P)).then_inc(s_ids, 16)
            sp.dma_start(dense_sb[:], dense_ctx.rearrange("(t p) f -> p t f", p=P)).then_inc(s_dense, 16)
            full = F * MAPS // P
            for l in (1, 2):
                flat = cin_w[l].rearrange("h k s -> (h k) s")
                dst = staged[:, RAW[l]:RAW[l] + full * S_OUT].rearrange("p (t s) -> p t s", s=S_OUT)
                sp.dma_start(dst, flat[0:full * P, :].rearrange("(t p) s -> p t s", p=P)).then_inc(s_wraw, 16)
                sp.dma_start(raw(l, full, F * MAPS - full * P), flat[full * P:, :]).then_inc(s_wraw, 16)

            def load_x0a(b):
                for j in range(SH_PER):
                    sp.dma_start(x0a[j * F:(j + 1) * F, :], block_rows(b)[F:2 * F, :]).then_inc(s_x0a, 16)

            def load_x0b(b, t):
                for j in range(ROWS[0][t] // F):
                    shift = (SH_PER * t + j + 1) % SHIFTS
                    row = shift or F
                    sp.dma_start(x0b[j * F:(j + 1) * F, t % B_RING, :],
                                 block_rows(b)[row:row + F, :]).then_inc(s_x0b[t % B_RING], 16)

            def load_x0rep(b, t):
                for j in range(ROWS[1][t] // MAPS):
                    h = 2 * t + j or F
                    row = block_rows(b)[h:h + 1, :]
                    sp.dma_start(x0rep[j * MAPS:(j + 1) * MAPS, t, :],
                                 row.broadcast_to((MAPS, COLS))).then_inc(s_x0rep[t], 16)

            def heads(b):
                load_x0a(b)
                for t in range(B_RING):
                    load_x0b(b, t)

            sp.wait_ge(s_dram, 4 * 16)
            heads(0)
            sp.wait_ge(s_wcopy, n_whole)
            sp.wait_ge(s_whigh, n_split)
            sp.wait_ge(s_wlow, n_split)
            for t in range(TILES[1]):
                load_x0rep(0, t)
                if t + B_RING < TILES[0]:
                    sp.wait_ge(s_prod, t + 1)
                    load_x0b(0, t + B_RING)
            sp.wait_ge(s_prod, TILES[0])
            heads(1)

            def one_half(first, b, dram_tiles):
                for t in range(B_RING, TILES[0]):
                    sp.wait_ge(s_prod, first + t - B_RING + 1)
                    load_x0b(b + 1, t)
                for t in range(TILES[1]):
                    sp.wait_ge(s_prod, first + TILES[0] + t + 1)
                    load_x0rep(b + 1, t)
                if dram_tiles is not None:
                    sp.wait_ge(s_dram, dram_tiles * 64)
                    heads(b + 2)

            with sp.Fori(0, BT - 1) as bt:
                one_half(PRO + bt * BODY, bt * 2, bt + 2)
                one_half(PRO + HALF + bt * BODY, bt * 2 + 1, bt + 2)
            one_half(PRO + (BT - 1) * BODY, NB - 2, None)
            sp.wait_ge(s_mlp_act, 2 * (H1 // P + H2 // P + 1))
            sp.dma_start(out.rearrange("b o -> o b"), y_sb[:]).then_inc(s_out, 16)
            sp.wait_ge(s_out, 16)

        @blk.gpsimd
        def _(pool):
            pool.wait_ge(s_ids, 16)

            def gather(t, column):
                for f in range(F):
                    pool.indirect_dma_start(
                        emb[:, f, :], None, tables[f],
                        bass.IndirectOffsetOnAxis(ap=column(f), axis=0)).then_inc(s_gather, 16)

            for t in range(BT):
                if t:
                    pool.wait_ge(s_turned, t * D // 4)
                gather(t, lambda f: ids_sb[:, t, f:f + 1])
                if t == 0:
                    pool.memset(ident[:], 0.0).then_inc(s_ident, 1)
                    pool.wait_ge(s_ident, 1)
                    pool.affine_select(out=ident[:], in_=ident[:], compare_op=ALU.not_equal, fill=1.0,
                                       base=0, pattern=[[-1, P]], channel_multiplier=1).then_inc(s_ident, 1)

        @blk.scalar
        def _(act):
            act.wait_ge(s_zero, 1)
            flat = cin_w[0].rearrange("h k s -> (h k) s")
            for g in range(SHIFTS):
                shift = (g + 1) % SHIFTS
                t, j = divmod(g, SH_PER)
                for a, n, wrap in ((0, F - shift, 0), (F - shift, shift, F)):
                    if not n:
                        continue
                    rows = slice(j * F + a, j * F + a + n)
                    h, k = a, a + shift - wrap
                    act.dma_start(staged[rows, RAW[0] + t * S_OUT:RAW[0] + (t + 1) * S_OUT],
                                  bass.AP(flat.tensor, (h * F + k) * S_OUT, [[(F + 1) * S_OUT, n], [1, S_OUT]])
                                  ).then_inc(s_wraw, 16)
                    if shift:
                        act.dma_start(staged[rows, RAW_T + t * S_OUT:RAW_T + (t + 1) * S_OUT],
                                      bass.AP(flat.tensor, (k * F + h) * S_OUT, [[(F + 1) * S_OUT, n], [1, S_OUT]])
                                      ).then_inc(s_wraw, 16)
            for l in range(3):
                act.dma_start(bias[:, l:l + 1], cin_b[l].rearrange("(p o) -> p o", o=1)).then_inc(s_bias, 16)
            for m in range(H1 // P):
                act.dma_start(bias[:, 3 + m:4 + m],
                              b_top1[m * P:(m + 1) * P].rearrange("(p o) -> p o", o=1)).then_inc(s_bias, 16)
            for m in range(H2 // P):
                act.dma_start(bias[:, 3 + H1 // P + m:4 + H1 // P + m],
                              b_top2[m * P:(m + 1) * P].rearrange("(p o) -> p o", o=1)).then_inc(s_bias, 16)
            act.dma_start(wt1[0:64, 0, :], W_top1[64:128, :]).then_inc(s_mlpw, 16)
            act.dma_start(wt1[64:128, 0, :], W_top1[0:64, :]).then_inc(s_mlpw, 16)
            act.dma_start(wt1[:, 1, :], W_top1[128:256, :]).then_inc(s_mlpw, 16)
            act.dma_start(wt1[0:DENSE, 2, :], W_top1[256:256 + DENSE, :]).then_inc(s_mlpw, 16)
            act.dma_start(wt2[:], W_top2.rearrange("(c p) m -> p c m", p=P)).then_inc(s_mlpw, 16)
            for c in range(H2 // P):
                act.dma_start(wt3[:, c:c + 1], W_top3[c * P:(c + 1) * P, :]).then_inc(s_mlpw, 16)

            act.wait_ge(s_wraw, 16 * N_WRAW)
            act.wait_ge(s_wsum, 1)
            for l in range(3):
                for t in SPLIT[l]:
                    r = ROWS[l][t]
                    act.activation(w_high[0:r, w_at[l, t], :], raw(l, t, r), ACT.Copy).then_inc(s_whigh, 1)

            act.wait_ge(s_dense_turned, 1)
            act.activation(dense_t[:], spare[0][0:DENSE, 0:B], ACT.Copy).then_inc(s_dense_copied, 1)

            def copy_x0t(r, before):
                act.wait_ge(s_turned, before + r + 1)
                act.activation(x0t[:, :, 4 * r:4 * r + 4, :].rearrange("p i d b -> p d i b"),
                               spare[r % 2][0:F, :].rearrange("p (d i b) -> p d i b", d=4, i=2),
                               ACT.Copy).then_inc(s_x0t, 1)

            def write_x0(bt, rounds):
                act.wait_ge(s_x0t, rounds)
                for i in range(2):
                    for twice in range(2):
                        act.dma_start(block_rows(bt * 2 + i)[twice * F:(twice + 1) * F, :],
                                      x0t[:, i].rearrange("p d b -> p (d b)")).then_inc(s_dram, 16)

            for r in range(D // 4):
                copy_x0t(r, 0)
            write_x0(0, D // 4)
            act.wait_ge(s_bias, 16 * (3 + H1 // P + H2 // P))

            def relu(dst, l, rows):
                return act.activation(dst, z[l][rows, :], ACT.Relu, bias=bias[rows, l:l + 1])

            def evacuate(l, number, b):
                act.wait_ge(s_tile, number + 1)
                maps, rest = slice(0, MAPS), slice(MAPS, P)
                if l < 2:
                    relu(xk[l + 1][maps, :], l, maps)
                    relu(xk[l + 1][rest, :], l, maps).then_inc(s_xk[l + 1], 1)
                    if not isinstance(b, int) or b:
                        act.wait_ge(s_sum01, b)
                    relu(direct01[rest if l == 0 else maps, :], l, rest).then_inc(s_read[l], 1)
                else:
                    relu(direct2[:], l, slice(0, P)).then_inc(s_read[l], 1)

            def tiles(kind, bt=None):
                jobs, first, first_s, b0, slot0, slot0_s = run(kind, bt)
                for pos, l, t, db, o in walk(jobs):
                    b = of_tail(kind, pos, db, b0)
                    if kind == "tail" and l == 2 and db == 1 and t == 0:
                        mlp_part(0, 0, MAIN)
                    if o is not None:
                        act.wait_ge(s_prod, first + pos + 1)
                        if o >= HALF_RING:
                            users = [q for q, _, _, _, u in walk(jobs) if u == o - HALF_RING]
                            act.wait_ge(s_tile, first + users[0] + 1)
                        elif kind != "prologue":
                            act.wait_ge(s_tile, first)
                        act.activation(high[0:ROWS[l][t], (slot0_s + o) % HALF_RING, :],
                                       prod[0:ROWS[l][t], (slot0 + pos) % P_RING, :], ACT.Copy).then_inc(s_high, 1)
                    if last_of(l, t):
                        evacuate(l, first + pos, b)
                    if kind == "body" and pos in TURN_AT:
                        r = TURN_AT[pos]
                        if r == 0:
                            act.wait_ge(s_dram, (bt + 1) * 64)
                        copy_x0t(r, (bt + 1) * (D // 4))
                        if r == D // 4 - 1:
                            write_x0(bt + 1, (bt + 2) * (D // 4))

            def mlp_part(part, c0, n):
                done = part * MLP_STEPS
                for m in range(H1 // P):
                    act.wait_ge(s_mlp_mm, done + m + 1)
                    act.activation(h1[:, m, 0:n], spare[m % 2][:, 0:n], ACT.Relu,
                                   bias=bias[:, 3 + m:4 + m]).then_inc(s_mlp_act, 1)
                for m in range(H2 // P):
                    q = H1 // P + m
                    act.wait_ge(s_mlp_mm, done + q + 1)
                    act.activation(h2[:, m, 0:n], spare[q % 2][:, 0:n], ACT.Relu,
                                   bias=bias[:, 3 + q:4 + q]).then_inc(s_mlp_act, 1)
                q = MLP_STEPS - 1
                act.wait_ge(s_mlp_mm, done + q + 1)
                act.activation(y_sb[:, c0:c0 + n], spare[q % 2][0:1, 0:n], ACT.Copy).then_inc(s_mlp_act, 1)

            tiles("prologue")
            with act.Fori(0, BT - 1) as bt:
                tiles("body", bt)
            tiles("tail", BT - 1)
            mlp_part(1, MAIN, BB)

        @blk.vector
        def _(dve):
            dve.memset(staged[:, RAW[0]:RAW_T + TILES[0] * S_OUT], 0.0).then_inc(s_zero, 1)
            dve.wait_ge(s_wraw, 16 * N_WRAW)
            n = TILES[0] * S_OUT
            dve.tensor_tensor(staged[:, RAW[0]:RAW[0] + n], staged[:, RAW[0]:RAW[0] + n],
                              staged[:, RAW_T:RAW_T + n], ALU.add).then_inc(s_wsum, 1)
            dve.wait_ge(s_wsum, 1)
            for l in range(3):
                for t in whole_of[l]:
                    r = ROWS[l][t]
                    dve.tensor_copy(w_whole[0:r, w_at[l, t], :], raw(l, t, r)).then_inc(s_wcopy, 1)
            made = 0
            for l in range(3):
                for t in SPLIT[l]:
                    r, made = ROWS[l][t], made + 1
                    dve.wait_ge(s_whigh, made)
                    dve.tensor_tensor(w_low[0:r, w_at[l, t], :], raw(l, t, r),
                                      w_high[0:r, w_at[l, t], :].bitcast(F32), ALU.subtract).then_inc(s_wlow, 1)

            def sum01(b):
                dve.wait_ge(s_read[1], b + 1)
                dve.wait_ge(s_read[0], b + 1)
                dve.tensor_reduce(columns(0, b), direct01[:].rearrange("p (d b) -> p b d", d=D),
                                  AX_X, ALU.add).then_inc(s_sum01, 1)

            def sum2(b):
                dve.wait_ge(s_read[2], b + 1)
                dve.tensor_reduce(columns(1, b), direct2[:].rearrange("p (d b) -> p b d", d=D),
                                  AX_X, ALU.add).then_inc(s_sum2, 1)

            def columns(part, b):
                return sums[:, part, b * BB:(b + 1) * BB] if isinstance(b, int) else sums[:, part, bass.ds(b * BB, BB)]

            def tiles(kind, bt=None):
                jobs, first, first_s, b0, slot0, slot0_s = run(kind, bt)
                lows = []
                for pos, l, t, db, o in walk(jobs):
                    b = of_tail(kind, pos, db, b0)
                    rows, slot = ROWS[l][t], (slot0 + pos) % P_RING
                    dst = prod[0:rows, slot, :]
                    if kind != "prologue" or pos >= P_RING:
                        user = pos - P_RING
                        if user < 0:
                            user = next(q for q in range(-1, -BODY, -1) if (q + BODY) % P_RING == slot)
                        dve.wait_ge(s_tile, first + user + 1)
                    if l == 0:
                        if t == 0:
                            dve.wait_ge(s_x0a, (b + 1) * 16 * SH_PER)
                        slot_b = t % B_RING
                        per = sum(ROWS[0][q] // F for q in range(slot_b, TILES[0], B_RING))
                        now = sum(ROWS[0][q] // F for q in range(slot_b, t + 1, B_RING))
                        dve.wait_ge(s_x0b[slot_b], (b * per + now) * 16)
                        dve.tensor_tensor(dst, x0a[0:rows, :], x0b[0:rows, slot_b, :], ALU.mult).then_inc(s_prod, 1)
                    else:
                        if t == 0:
                            dve.wait_ge(s_xk[l], b + 1)
                        if l == 1:
                            dve.wait_ge(s_x0rep[t], (b + 1) * 16 * (rows // MAPS))
                        dve.tensor_tensor(dst, x0rep[0:rows, t, :], xk[l][0:rows, :], ALU.mult).then_inc(s_prod, 1)
                    if o is not None:
                        end = pos + TILES[l] - 1 - t if kind == "prologue" or l == 1 else len(jobs) - 1
                        lows.append((min(pos + LOW_LAG, end), (pos, l, t, o)))
                    while lows and lows[0][0] <= pos:
                        low_part(jobs, first, first_s, slot0, slot0_s, kind, *lows.pop(0)[1])
                    if kind != "prologue" and t == SUM_AT:
                        if l == 0:
                            sum01(b - 1)
                        if l == 1:
                            sum2(b - 1)
                        if kind == "tail" and l == 2 and db == 1:
                            sum01(b)

            def low_part(jobs, first, first_s, slot0, slot0_s, kind, pos, l, t, o):
                rows, slot_s = ROWS[l][t], (slot0_s + o) % HALF_RING
                dve.wait_ge(s_high, first_s + o + 1)
                if o >= HALF_RING:
                    users = [q for q, _, _, _, u in walk(jobs) if u == o - HALF_RING]
                    dve.wait_ge(s_tile, first + users[0] + 1)
                elif kind != "prologue":
                    dve.wait_ge(s_tile, first)
                dve.tensor_tensor(low[0:rows, slot_s, :], prod[0:rows, (slot0 + pos) % P_RING, :],
                                  high[0:rows, slot_s, :].bitcast(F32), ALU.subtract).then_inc(s_low, 1)

            tiles("prologue")
            with dve.Fori(0, BT - 1) as bt:
                tiles("body", bt)
            tiles("tail", BT - 1)
            sum2(NB - 1)

        @blk.tensor
        def _(pe):
            pe.wait_ge(s_ident, 2)
            pe.wait_ge(s_dense, 16)
            for t in range(BT):
                mm = pe.transpose(spare[0][0:DENSE, t * P:(t + 1) * P], dense_sb[:, t, :], ident[:])
            mm.then_inc(s_dense_turned, 1)
            pe.wait_ge(s_dense_copied, 1)

            def turn(r):
                for i in range(4):
                    mm = pe.transpose(spare[r % 2][0:F, i * P:(i + 1) * P], emb[:, :, 4 * r + i], ident[:])
                mm.then_inc(s_turned, 1)

            pe.wait_ge(s_gather, 16 * F)
            for r in range(D // 4):
                if r >= 2:
                    pe.wait_ge(s_x0t, r - 1)
                turn(r)
            pe.wait_ge(s_wcopy, n_whole)
            pe.wait_ge(s_whigh, n_split)
            pe.wait_ge(s_wlow, n_split)

            def tiles(kind, bt=None):
                jobs, first, first_s, b0, slot0, slot0_s = run(kind, bt)
                for pos, l, t, db, o in walk(jobs):
                    b = of_tail(kind, pos, db, b0)
                    if kind == "tail" and l == 2 and db == 1 and t == 0:
                        mlp_part(0, 0, MAIN)
                    if t == 0:
                        if l == 2:
                            pe.wait_ge(s_xk[2], b + 1)
                        elif not isinstance(b, int) or b:
                            pe.wait_ge(s_read[l], b)
                    if kind == "body" and pos in TURN_AT:
                        r = TURN_AT[pos]
                        if r == 0:
                            pe.wait_ge(s_gather, (bt + 2) * (16 * F))
                        pe.wait_ge(s_x0t, bt * (D // 4) + (D // 4 + r - 1))
                    rows = ROWS[l][t]
                    start, stop = t == 0, last_of(l, t)
                    w = w_at[l, t]
                    if o is None:
                        pe.wait_ge(s_prod, first + pos + 1)
                        for c in range(CH):
                            cols = slice(c * BANK, (c + 1) * BANK)
                            mm = pe.matmul(z[l][:, cols], w_whole[0:rows, w, :],
                                           prod[0:rows, (slot0 + pos) % P_RING, cols], start=start, stop=stop)
                    else:
                        slot = (slot0_s + o) % HALF_RING
                        pe.wait_ge(s_high, first_s + o + 1)
                        for weights in (w_high, w_low):
                            for c in range(CH):
                                cols = slice(c * BANK, (c + 1) * BANK)
                                pe.matmul(z[l][:, cols], weights[0:rows, w, :], high[0:rows, slot, cols],
                                          start=start and weights is w_high, stop=False)
                        pe.wait_ge(s_low, first_s + o + 1)
                        for c in range(CH):
                            cols = slice(c * BANK, (c + 1) * BANK)
                            mm = pe.matmul(z[l][:, cols], w_high[0:rows, w, :], low[0:rows, slot, cols],
                                           start=False, stop=stop)
                    mm.then_inc(s_tile, 1)
                    if kind == "body" and pos in TURN_AT:
                        turn(TURN_AT[pos])

            def mlp_part(part, c0, n):
                done = part * MLP_STEPS
                if part == 0:
                    pe.wait_ge(s_mlpw, 16 * N_MLPW)
                    pe.wait_ge(s_x0t, BT * (D // 4))
                    pe.wait_ge(s_sum2, NB - 1)
                    pe.wait_ge(s_sum01, NB - 1)
                else:
                    pe.wait_ge(s_sum01, NB)
                    pe.wait_ge(s_sum2, NB)

                def free(q):
                    if done + q >= 2:
                        pe.wait_ge(s_mlp_act, done + q - 1)

                for m in range(H1 // P):
                    free(m)
                    ms = slice(m * P, (m + 1) * P)
                    o = spare[m % 2][:, 0:n]
                    pe.matmul(o, wt1[0:DENSE, 2, ms], dense_t[:, c0:c0 + n], start=True, stop=False)
                    pe.matmul(o, wt1[:, 0, ms], sums[:, 0, c0:c0 + n], start=False, stop=False)
                    pe.matmul(o, wt1[:, 1, ms], sums[:, 1, c0:c0 + n], start=False, stop=True).then_inc(s_mlp_mm, 1)
                for m in range(H2 // P):
                    q = H1 // P + m
                    free(q)
                    for c in range(H1 // P):
                        pe.wait_ge(s_mlp_act, done + c + 1)
                        mm = pe.matmul(spare[q % 2][:, 0:n], wt2[:, c, m * P:(m + 1) * P], h1[:, c, 0:n],
                                       start=(c == 0), stop=(c == H1 // P - 1))
                    mm.then_inc(s_mlp_mm, 1)
                q = MLP_STEPS - 1
                free(q)
                for c in range(H2 // P):
                    pe.wait_ge(s_mlp_act, done + H1 // P + c + 1)
                    mm = pe.matmul(spare[q % 2][0:1, 0:n], wt3[:, c:c + 1], h2[:, c, 0:n],
                                   start=(c == 0), stop=(c == H2 // P - 1))
                mm.then_inc(s_mlp_mm, 1)

            tiles("prologue")
            with pe.Fori(0, BT - 1) as bt:
                tiles("body", bt)
            tiles("tail", BT - 1)
            mlp_part(1, MAIN, BB)


SUM_AT = 3
TURN_AT = {7 + 20 + r: r for r in range(4)}
MLP_STEPS = 4 + 2 + 1
N_MLPW = 7
N_WRAW = 4 + 2 * 2 * 19 + 1


def kernel(**inputs):
    import numpy as _np
    import concourse.bacc as _bacc
    from concourse import mybir as _mybir
    from concourse.bass_utils import run_bass_kernel_spmd as _run

    nc = _bacc.Bacc("TRN2", target_bir_lowering=False, num_devices=1)
    arrays = {}

    def given(name):
        a = _np.ascontiguousarray(inputs[name])
        arrays[f"in_{name}_dram"] = a
        return nc.dram_tensor(f"in_{name}_dram", a.shape, _mybir.dt.from_np(a.dtype), kind="ExternalInput").ap()

    n_tables = inputs["ids"].shape[1]
    out = nc.dram_tensor("out_0_dram", (inputs["ids"].shape[0], 1), _mybir.dt.float32, kind="ExternalOutput").ap()
    cin_tower(nc, given("dense_ctx"), given("ids"), [given(f"tbl_{i}") for i in range(n_tables)],
              given("W_top1"), given("b_top1"), given("W_top2"), given("b_top2"), given("W_top3"),
              [given(f"L0_rec_w{i}") for i in range(3)], [given(f"L0_rec_b{i}") for i in range(3)], out)
    r = _run(nc, [arrays], core_ids=[0])
    return r.results[0]["out_0_dram"]
```

```python
from contextlib import ExitStack

import concourse.bass as bass
from concourse import mybir

F32 = mybir.dt.float32
F32R = mybir.dt.float32r
I32 = mybir.dt.int32
ALU = mybir.AluOpType
ACT = mybir.ActivationFunctionType
AX_X = mybir.AxisListType.X

P = 128
SPLIT = {0: (4,), 1: (4, 6, 9, 11, 14, 16, 18), 2: (4, 7, 9, 12, 14, 17, 19)}
P_RING, HALF_RING, B_RING = 6, 2, 4
LOW_LAG = 2


def cin_tower(nc, dense_ctx, ids, tables, W_top1, b_top1, W_top2, b_top2, W_top3, cin_w, cin_b, out):
    B, DENSE = dense_ctx.shape
    F = len(tables)
    D = tables[0].shape[1]
    S_OUT = cin_w[0].shape[2]
    MAPS = cin_w[1].shape[1]
    H1, H2 = W_top1.shape[1], W_top2.shape[1]

    BT = B // P
    BB = P // 2
    NB = B // BB
    COLS = BB * D
    BANK = 512
    CH = COLS // BANK

    SHIFTS = F // 2 + 1
    SH_PER = P // F
    TILES = {0: -(-SHIFTS // SH_PER), 1: -(-F * MAPS // P), 2: -(-F * MAPS // P)}
    ROWS = {0: [F * SH_PER] * TILES[0]}
    ROWS[1] = ROWS[2] = [min(P, F * MAPS - P * t) for t in range(TILES[1])]
    assert B % P == 0 and MAPS == 64 and S_OUT == P and F % 2 == 1 and D == 16

    def layer(l, db):
        return [(l, t, db) for t in range(TILES[l])]

    half = layer(0, 1) + layer(2, 0) + layer(1, 1)
    prologue = layer(0, 0) + layer(1, 0)
    body = half + half
    tail = half + layer(2, 1)
    PRO, BODY, HALF = len(prologue), len(body), len(half)

    def splits(jobs):
        return sum(t in SPLIT[l] for l, t, _ in jobs)

    PRO_S, BODY_S = splits(prologue), splits(body)
    assert BODY_S % HALF_RING == 0

    whole_of = {l: [t for t in range(TILES[l]) if t not in SPLIT[l]] for l in range(3)}
    w_at, n_whole, n_split = {}, 0, 0
    for l in range(3):
        for t in range(TILES[l]):
            if t in SPLIT[l]:
                w_at[l, t], n_split = n_split, n_split + 1
            else:
                w_at[l, t], n_whole = n_whole, n_whole + 1

    with ExitStack() as ctx:
        def sb(name, shape, dt=F32):
            return ctx.enter_context(nc.sbuf_tensor(name, shape, dt))

        def psum(name, shape):
            return ctx.enter_context(nc.psum_tensor(name, shape, F32))

        def sem(name):
            return ctx.enter_context(nc.semaphore(name))

        x0rep = sb("x0rep", [P, TILES[1], COLS])
        staged = x0rep[:].rearrange("p t c -> p (t c)")
        w_whole = sb("w_whole", [P, n_whole, S_OUT])
        w_high = sb("w_high", [P, n_split, S_OUT], F32R)
        w_low = sb("w_low", [P, n_split, S_OUT], F32R)
        prod = sb("prod", [P, P_RING, COLS])
        high = sb("high", [P, HALF_RING, COLS], F32R)
        low = sb("low", [P, HALF_RING, COLS], F32R)
        xk = {1: sb("xk1", [P, COLS]), 2: sb("xk2", [P, COLS])}
        x0a = sb("x0a", [P, COLS])
        x0b = sb("x0b", [P, B_RING, COLS])
        direct01 = sb("direct01", [P, COLS])
        direct2 = sb("direct2", [P, COLS])
        emb = sb("emb", [P, F, D])
        x0t = sb("x0t", [F, 2, D, BB])
        ids_sb = sb("ids_sb", [P, BT, F], I32)
        ident = sb("ident", [P, P])
        sums = sb("sums", [P, 2, B])
        dense_sb = sb("dense_sb", [P, BT, DENSE])
        dense_t = sb("dense_t", [DENSE, B])
        wt_dense = sb("wt_dense", [DENSE, H1])
        wt3 = sb("wt3", [P, H2 // P])
        bias = sb("bias", [P, 3 + H1 // P + H2 // P])
        MAIN = B - BB
        y_sb = emb[0:1].rearrange("p f d -> p (f d)")[:, 0:B]
        wt2 = x0a[:].rearrange("p (c m) -> p c m", m=H2)
        mlp = x0b[:].rearrange("p r c -> p (r c)")
        h1 = mlp[:, 0:H1 // P * MAIN].rearrange("p (m n) -> p m n", n=MAIN)
        h2 = mlp[:, H1 // P * MAIN:(H1 + H2) // P * MAIN].rearrange("p (m n) -> p m n", n=MAIN)
        wt1 = mlp[:, B_RING * COLS - 2 * H1:].rearrange("p (c m) -> p c m", m=H1)
        assert H1 // P * H2 == COLS and (H1 + H2) // P * MAIN + 2 * H1 <= B_RING * COLS

        z = [psum(f"z{l}", [P, COLS]) for l in range(3)]
        spare = [psum(f"spare{i}", [P, BANK]) for i in range(2)]

        w0_cols = nc.dram_tensor("w0_cols", (F, 2 * F, S_OUT), F32, kind="Internal").ap()
        w0_rows = nc.dram_tensor("w0_rows", (2 * F, F, S_OUT), F32, kind="Internal").ap()
        x0_dram = nc.dram_tensor("x0_dram", (NB, 2 * F, COLS), F32, kind="Internal").ap()

        s_ids = sem("ids_loaded")
        s_dense = sem("dense_loaded")
        s_wdram = sem("w0_copied")
        s_wraw = sem("cin_weights_loaded")
        s_zero = sem("staging_zeroed")
        s_mlpw = sem("mlp_weights_loaded")
        s_bias = sem("biases_loaded")
        s_ident = sem("identity_made")
        s_wsum = sem("pair_weights_added")
        s_wcopy = sem("whole_weights_copied")
        s_whigh = sem("high_weights_made")
        s_wlow = sem("low_weights_made")
        s_gather = sem("rows_gathered")
        s_turned = sem("transposes_done")
        s_x0t = sem("x0t_copied")
        s_dram = sem("x0_written")
        s_x0a = sem("x0a_loaded")
        s_x0b = [sem(f"x0b{i}_loaded") for i in range(B_RING)]
        s_x0rep = [sem(f"x0rep{t}_loaded") for t in range(TILES[1])]
        s_prod = sem("products_done")
        s_high = sem("highs_done")
        s_low = sem("lows_done")
        s_tile = sem("tiles_contracted")
        s_xk = {1: sem("xk1_ready"), 2: sem("xk2_ready")}
        s_read = [sem(f"z{l}_evacuated") for l in range(3)]
        s_sum01 = sem("direct01_summed")
        s_sum2 = sem("direct2_summed")
        s_dense_turned = sem("dense_transposed")
        s_dense_copied = sem("dense_copied")
        s_mlp_mm = sem("mlp_matmuls_done")
        s_mlp_act = sem("mlp_activated")
        s_out = sem("out_written")

        def block_rows(b):
            if isinstance(b, int):
                return x0_dram[b]
            return x0_dram[bass.ds(b, 1), :, :].rearrange("o r c -> (o r) c")

        RAW = {1: 0, 2: TILES[1] * S_OUT, 0: 2 * TILES[1] * S_OUT}
        RAW_T = RAW[0] + TILES[0] * S_OUT

        def raw(l, t, rows):
            return staged[0:rows, RAW[l] + t * S_OUT:RAW[l] + (t + 1) * S_OUT]

        def walk(jobs):
            n = 0
            for pos, (l, t, db) in enumerate(jobs):
                split = t in SPLIT[l]
                yield pos, l, t, db, (n if split else None)
                n += split

        def run(kind, bt=None):
            if kind == "prologue":
                return prologue, 0, 0, 0, (BODY - PRO) % P_RING, (BODY_S - PRO_S) % HALF_RING
            jobs = body if kind == "body" else tail
            return jobs, PRO + bt * BODY, PRO_S + bt * BODY_S, bt * 2, 0, 0

        def block_of(pos, db, b0):
            return b0 + (pos // HALF) + db if pos < 2 * HALF else b0 + db

        def of_tail(kind, pos, db, b0):
            return b0 + db if kind == "tail" else block_of(pos, db, b0)

        def last_of(l, t):
            return t == TILES[l] - 1

        blk = ctx.enter_context(nc.Block())

        @blk.sync
        def _(sp):
            sp.dma_start(ids_sb[:], ids.rearrange("(t p) f -> p t f", p=P)).then_inc(s_ids, 16)
            sp.dma_start(dense_sb[:], dense_ctx.rearrange("(t p) f -> p t f", p=P)).then_inc(s_dense, 16)
            full = F * MAPS // P
            for l in (1, 2):
                flat = cin_w[l].rearrange("h k s -> (h k) s")
                dst = staged[:, RAW[l]:RAW[l] + full * S_OUT].rearrange("p (t s) -> p t s", s=S_OUT)
                sp.dma_start(dst, flat[0:full * P, :].rearrange("(t p) s -> p t s", p=P)).then_inc(s_wraw, 16)
                sp.dma_start(raw(l, full, F * MAPS - full * P), flat[full * P:, :]).then_inc(s_wraw, 16)

            def overlapped(b, row, step):
                rows = block_rows(b)[row:row + F, :]
                return bass.AP(rows.tensor, rows.offset, [[COLS, F], [step * COLS, SH_PER], [1, COLS]])

            def load_x0a(b):
                sp.dma_start(x0a[0:F * SH_PER, :], overlapped(b, F, 0)).then_inc(s_x0a, 16)

            def load_x0b(b, t):
                sp.dma_start(x0b[0:F * SH_PER, t % B_RING, :], overlapped(b, SH_PER * t, 1)
                             ).then_inc(s_x0b[t % B_RING], 16)

            def load_x0rep(b, t):
                for j in range(ROWS[1][t] // MAPS):
                    h = 2 * t + j or F
                    row = block_rows(b)[h:h + 1, :]
                    sp.dma_start(x0rep[j * MAPS:(j + 1) * MAPS, t, :],
                                 row.broadcast_to((MAPS, COLS))).then_inc(s_x0rep[t], 16)

            def heads(b):
                load_x0a(b)
                for t in range(B_RING):
                    load_x0b(b, t)

            def write_x0(bt, rounds):
                sp.wait_ge(s_x0t, rounds)
                for i in range(2):
                    for twice in (1, 0):
                        sp.dma_start(block_rows(bt * 2 + i)[twice * F:(twice + 1) * F, :],
                                     x0t[:, i].rearrange("p d b -> p (d b)")).then_inc(s_dram, 16)

            write_x0(0, D // 4)
            sp.wait_ge(s_dram, 4 * 16)
            heads(0)
            sp.wait_ge(s_wcopy, n_whole)
            sp.wait_ge(s_whigh, n_split)
            sp.wait_ge(s_wlow, n_split)
            for t in range(TILES[1]):
                load_x0rep(0, t)
                if t + B_RING < TILES[0]:
                    sp.wait_ge(s_prod, t + 1)
                    load_x0b(0, t + B_RING)
            sp.wait_ge(s_prod, TILES[0])
            heads(1)

            def one_half(first, b, turned):
                for t in range(B_RING, TILES[0]):
                    sp.wait_ge(s_prod, first + t - B_RING + 1)
                    load_x0b(b + 1, t)
                for t in range(TILES[1]):
                    sp.wait_ge(s_prod, first + TILES[0] + t + 1)
                    load_x0rep(b + 1, t)
                if turned is not None:
                    write_x0(turned, (turned + 1) * (D // 4))
                    sp.wait_ge(s_dram, (turned + 1) * 64)

            with nc.Fori(0, BT - 1, engines=[mybir.EngineType.SP], hint_back_edge=True) as bt:
                one_half(PRO + bt * BODY, bt * 2, bt + 1)
                heads(bt * 2 + 2)
                one_half(PRO + HALF + bt * BODY, bt * 2 + 1, None)
                heads(bt * 2 + 3)
            first = PRO + (BT - 1) * BODY
            one_half(first, NB - 2, None)
            sp.wait_ge(s_prod, first + TILES[0])
            direct = P - MAPS
            sp.dma_start(wt1[0:direct, 0, :], W_top1[direct:2 * direct, :]).then_inc(s_mlpw, 16)
            sp.dma_start(wt1[direct:P, 0, :], W_top1[0:direct, :]).then_inc(s_mlpw, 16)
            sp.dma_start(wt1[:, 1, :], W_top1[P:2 * P, :]).then_inc(s_mlpw, 16)
            sp.dma_start(wt2[:], W_top2.rearrange("(c p) m -> p c m", p=P)).then_inc(s_mlpw, 16)
            sp.wait_ge(s_mlp_act, 2 * (H1 // P + H2 // P + 1))
            sp.dma_start(out.rearrange("b o -> o b"), y_sb[:]).then_inc(s_out, 16)
            sp.wait_ge(s_out, 16)

        @blk.gpsimd
        def _(pool):
            pool.wait_ge(s_ids, 16)

            def gather(t, column):
                for f in range(F):
                    pool.indirect_dma_start(
                        emb[:, f, :], None, tables[f],
                        bass.IndirectOffsetOnAxis(ap=column(f), axis=0)).then_inc(s_gather, 16)

            for t in range(BT):
                if t:
                    pool.wait_ge(s_turned, t * D // 4)
                gather(t, lambda f: ids_sb[:, t, f:f + 1])
                if t == 0:
                    pool.memset(ident[:], 0.0).then_inc(s_ident, 1)
                    pool.wait_ge(s_ident, 1)
                    pool.affine_select(out=ident[:], in_=ident[:], compare_op=ALU.not_equal, fill=1.0,
                                       base=0, pattern=[[-1, P]], channel_multiplier=1).then_inc(s_ident, 1)

        @blk.scalar
        def _(act):
            act.dma_start(w0_cols[:, 0:F, :], cin_w[0]).then_inc(s_wdram, 16)
            act.dma_start(w0_cols[:, F:, :], cin_w[0]).then_inc(s_wdram, 16)
            act.dma_start(w0_rows[0:F], cin_w[0]).then_inc(s_wdram, 16)
            act.dma_start(w0_rows[F:], cin_w[0]).then_inc(s_wdram, 16)
            act.wait_ge(s_wdram, 4 * 16)
            act.wait_ge(s_zero, 1)

            def load_w0(t, js, at, src, per_h, per_k):
                apart = js if len(js) < SH_PER else [None]
                for j in apart:
                    rows, lo, n = (slice(0, F * SH_PER), 0, SH_PER) if j is None else (
                        slice(j, F * SH_PER, SH_PER), j, 1)
                    act.dma_start(staged[rows, at + t * S_OUT:at + (t + 1) * S_OUT],
                                  bass.AP(src.tensor, (SH_PER * t + lo) * per_k,
                                          [[per_h + per_k, F], [per_k, n], [1, S_OUT]])).then_inc(s_wraw, 16)

            for t in range(TILES[0]):
                js = [j for j in range(SH_PER) if SH_PER * t + j < SHIFTS]
                load_w0(t, js, RAW[0], w0_cols, 2 * F * S_OUT, S_OUT)
                load_w0(t, [j for j in js if t or j], RAW_T, w0_rows, S_OUT, F * S_OUT)
            for l in range(3):
                act.dma_start(bias[:, l:l + 1], cin_b[l].rearrange("(p o) -> p o", o=1)).then_inc(s_bias, 16)
            for m in range(H1 // P):
                act.dma_start(bias[:, 3 + m:4 + m],
                              b_top1[m * P:(m + 1) * P].rearrange("(p o) -> p o", o=1)).then_inc(s_bias, 16)
            for m in range(H2 // P):
                act.dma_start(bias[:, 3 + H1 // P + m:4 + H1 // P + m],
                              b_top2[m * P:(m + 1) * P].rearrange("(p o) -> p o", o=1)).then_inc(s_bias, 16)
            act.dma_start(wt_dense[:], W_top1[2 * P:2 * P + DENSE, :]).then_inc(s_mlpw, 16)
            for c in range(H2 // P):
                act.dma_start(wt3[:, c:c + 1], W_top3[c * P:(c + 1) * P, :]).then_inc(s_mlpw, 16)

            act.wait_ge(s_wraw, 16 * N_WRAW)
            act.wait_ge(s_wsum, 1)
            for l in range(3):
                for t in SPLIT[l]:
                    r = ROWS[l][t]
                    act.activation(w_high[0:r, w_at[l, t], :], raw(l, t, r), ACT.Copy).then_inc(s_whigh, 1)

            act.wait_ge(s_dense_turned, 1)
            act.activation(dense_t[:], spare[0][0:DENSE, 0:B], ACT.Copy).then_inc(s_dense_copied, 1)

            def copy_x0t(r, before):
                act.wait_ge(s_turned, before + r + 1)
                act.activation(x0t[:, :, 4 * r:4 * r + 4, :].rearrange("p i d b -> p d i b"),
                               spare[r % 2][0:F, :].rearrange("p (d i b) -> p d i b", d=4, i=2),
                               ACT.Copy).then_inc(s_x0t, 1)

            for r in range(D // 4):
                copy_x0t(r, 0)
            act.wait_ge(s_bias, 16 * (3 + H1 // P + H2 // P))

            def relu(dst, l, rows):
                return act.activation(dst, z[l][rows, :], ACT.Relu, bias=bias[rows, l:l + 1])

            def evacuate(l, number, b):
                act.wait_ge(s_tile, number + 1)
                maps, rest = slice(0, MAPS), slice(MAPS, P)
                if l < 2:
                    relu(xk[l + 1][maps, :], l, maps)
                    relu(xk[l + 1][rest, :], l, maps).then_inc(s_xk[l + 1], 1)
                    if not isinstance(b, int) or b:
                        act.wait_ge(s_sum01, b)
                    relu(direct01[rest if l == 0 else maps, :], l, rest).then_inc(s_read[l], 1)
                else:
                    relu(direct2[:], l, slice(0, P)).then_inc(s_read[l], 1)

            def tiles(kind, bt=None):
                jobs, first, first_s, b0, slot0, slot0_s = run(kind, bt)
                for pos, l, t, db, o in walk(jobs):
                    b = of_tail(kind, pos, db, b0)
                    if kind == "tail" and l == 2 and db == 1 and t == 0:
                        mlp_part(0, 0, MAIN)
                    if o is not None:
                        act.wait_ge(s_prod, first + pos + 1)
                        if o >= HALF_RING:
                            users = [q for q, _, _, _, u in walk(jobs) if u == o - HALF_RING]
                            act.wait_ge(s_tile, first + users[0] + 1)
                        elif kind != "prologue":
                            act.wait_ge(s_tile, first)
                        act.activation(high[0:ROWS[l][t], (slot0_s + o) % HALF_RING, :],
                                       prod[0:ROWS[l][t], (slot0 + pos) % P_RING, :], ACT.Copy).then_inc(s_high, 1)
                    if last_of(l, t):
                        evacuate(l, first + pos, b)
                    if kind == "body" and pos - COPY_LAG in TURN_AT:
                        r = TURN_AT[pos - COPY_LAG]
                        if r == 0:
                            act.wait_ge(s_dram, (bt + 1) * 64)
                        copy_x0t(r, (bt + 1) * (D // 4))

            def mlp_part(part, c0, n):
                done = part * MLP_STEPS
                for m in range(H1 // P):
                    act.wait_ge(s_mlp_mm, done + m + 1)
                    act.activation(h1[:, m, 0:n], spare[m % 2][:, 0:n], ACT.Relu,
                                   bias=bias[:, 3 + m:4 + m]).then_inc(s_mlp_act, 1)
                for m in range(H2 // P):
                    q = H1 // P + m
                    act.wait_ge(s_mlp_mm, done + q + 1)
                    act.activation(h2[:, m, 0:n], spare[q % 2][:, 0:n], ACT.Relu,
                                   bias=bias[:, 3 + q:4 + q]).then_inc(s_mlp_act, 1)
                q = MLP_STEPS - 1
                act.wait_ge(s_mlp_mm, done + q + 1)
                act.activation(y_sb[:, c0:c0 + n], spare[q % 2][0:1, 0:n], ACT.Copy).then_inc(s_mlp_act, 1)

            tiles("prologue")
            with nc.Fori(0, BT - 1, engines=[mybir.EngineType.Activation], hint_back_edge=True) as bt:
                tiles("body", bt)
            tiles("tail", BT - 1)
            mlp_part(1, MAIN, BB)

        @blk.vector
        def _(dve):
            dve.memset(staged[:, RAW[0]:RAW_T + TILES[0] * S_OUT], 0.0).then_inc(s_zero, 1)
            dve.wait_ge(s_wraw, 16 * N_WRAW)
            n = TILES[0] * S_OUT
            dve.tensor_tensor(staged[:, RAW[0]:RAW[0] + n], staged[:, RAW[0]:RAW[0] + n],
                              staged[:, RAW_T:RAW_T + n], ALU.add).then_inc(s_wsum, 1)
            dve.wait_ge(s_wsum, 1)
            for l in range(3):
                for t in whole_of[l]:
                    r = ROWS[l][t]
                    dve.tensor_copy(w_whole[0:r, w_at[l, t], :], raw(l, t, r)).then_inc(s_wcopy, 1)
            made = 0
            for l in range(3):
                for t in SPLIT[l]:
                    r, made = ROWS[l][t], made + 1
                    dve.wait_ge(s_whigh, made)
                    dve.tensor_tensor(w_low[0:r, w_at[l, t], :], raw(l, t, r),
                                      w_high[0:r, w_at[l, t], :].bitcast(F32), ALU.subtract).then_inc(s_wlow, 1)

            def sum01(b):
                dve.wait_ge(s_read[1], b + 1)
                dve.wait_ge(s_read[0], b + 1)
                dve.tensor_reduce(columns(0, b), direct01[:].rearrange("p (d b) -> p b d", d=D),
                                  AX_X, ALU.add).then_inc(s_sum01, 1)

            def sum2(b):
                dve.wait_ge(s_read[2], b + 1)
                dve.tensor_reduce(columns(1, b), direct2[:].rearrange("p (d b) -> p b d", d=D),
                                  AX_X, ALU.add).then_inc(s_sum2, 1)

            def columns(part, b):
                return sums[:, part, b * BB:(b + 1) * BB] if isinstance(b, int) else sums[:, part, bass.ds(b * BB, BB)]

            def tiles(kind, bt=None):
                jobs, first, first_s, b0, slot0, slot0_s = run(kind, bt)
                lows = []
                for pos, l, t, db, o in walk(jobs):
                    b = of_tail(kind, pos, db, b0)
                    rows, slot = ROWS[l][t], (slot0 + pos) % P_RING
                    dst = prod[0:rows, slot, :]
                    if kind != "prologue" or pos >= P_RING:
                        user = pos - P_RING
                        if user < 0:
                            user = next(q for q in range(-1, -BODY, -1) if (q + BODY) % P_RING == slot)
                        if (jobs if user >= 0 else body)[user][1] in SPLIT[(jobs if user >= 0 else body)[user][0]]:
                            n = splits(jobs[:user + 1]) if user >= 0 else -splits(body[user + 1:])
                            dve.wait_ge(s_low, first_s + n)
                        else:
                            dve.wait_ge(s_tile, first + user + 1)
                    if l == 0:
                        if t == 0:
                            dve.wait_ge(s_x0a, (b + 1) * 16)
                        slot_b = t % B_RING
                        per = len(range(slot_b, TILES[0], B_RING))
                        now = t // B_RING + 1
                        dve.wait_ge(s_x0b[slot_b], (b * per + now) * 16)
                        dve.tensor_tensor(dst, x0a[0:rows, :], x0b[0:rows, slot_b, :], ALU.mult).then_inc(s_prod, 1)
                    else:
                        if t == 0:
                            dve.wait_ge(s_xk[l], b + 1)
                        if l == 1:
                            dve.wait_ge(s_x0rep[t], (b + 1) * 16 * (rows // MAPS))
                        dve.tensor_tensor(dst, x0rep[0:rows, t, :], xk[l][0:rows, :], ALU.mult).then_inc(s_prod, 1)
                    if o is not None:
                        end = pos + TILES[l] - 1 - t if kind == "prologue" or l == 1 else len(jobs) - 1
                        lows.append((min(pos + LOW_LAG, end), (pos, l, t, o)))
                    while lows and lows[0][0] <= pos:
                        low_part(jobs, first, first_s, slot0, slot0_s, kind, *lows.pop(0)[1])
                    if kind != "prologue" and t == SUM_AT[l]:
                        if l == 0:
                            sum01(b - 1)
                        if l == 1:
                            sum2(b - 1)
                        if kind == "tail" and l == 2 and db == 1:
                            sum01(b)

            def low_part(jobs, first, first_s, slot0, slot0_s, kind, pos, l, t, o):
                rows, slot_s = ROWS[l][t], (slot0_s + o) % HALF_RING
                dve.wait_ge(s_high, first_s + o + 1)
                if o >= HALF_RING:
                    users = [q for q, _, _, _, u in walk(jobs) if u == o - HALF_RING]
                    dve.wait_ge(s_tile, first + users[0] + 1)
                elif kind != "prologue":
                    dve.wait_ge(s_tile, first)
                dve.tensor_tensor(low[0:rows, slot_s, :], prod[0:rows, (slot0 + pos) % P_RING, :],
                                  high[0:rows, slot_s, :].bitcast(F32), ALU.subtract).then_inc(s_low, 1)

            tiles("prologue")
            with nc.Fori(0, BT - 1, engines=[mybir.EngineType.DVE], hint_back_edge=True) as bt:
                tiles("body", bt)
            tiles("tail", BT - 1)
            sum2(NB - 1)

        @blk.tensor
        def _(pe):
            pe.wait_ge(s_ident, 2)
            pe.wait_ge(s_dense, 16)
            for t in range(BT):
                mm = pe.transpose(spare[0][0:DENSE, t * P:(t + 1) * P], dense_sb[:, t, :], ident[:])
            mm.then_inc(s_dense_turned, 1)
            pe.wait_ge(s_dense_copied, 1)

            def turn(r):
                for i in range(4):
                    mm = pe.transpose(spare[r % 2][0:F, i * P:(i + 1) * P], emb[:, :, 4 * r + i], ident[:])
                mm.then_inc(s_turned, 1)

            pe.wait_ge(s_gather, 16 * F)
            for r in range(D // 4):
                if r >= 2:
                    pe.wait_ge(s_x0t, r - 1)
                turn(r)
            pe.wait_ge(s_wcopy, n_whole)
            pe.wait_ge(s_whigh, n_split)
            pe.wait_ge(s_wlow, n_split)

            def tiles(kind, bt=None):
                jobs, first, first_s, b0, slot0, slot0_s = run(kind, bt)
                for pos, l, t, db, o in walk(jobs):
                    b = of_tail(kind, pos, db, b0)
                    if kind == "tail" and l == 2 and db == 1 and t == 0:
                        mlp_part(0, 0, MAIN)
                    if t == 0:
                        if l == 2:
                            pe.wait_ge(s_xk[2], b + 1)
                        elif not isinstance(b, int) or b:
                            pe.wait_ge(s_read[l], b)
                    if kind == "body" and pos in TURN_AT:
                        r = TURN_AT[pos]
                        if r == 0:
                            pe.wait_ge(s_gather, (bt + 2) * (16 * F))
                        pe.wait_ge(s_x0t, bt * (D // 4) + (D // 4 + r - 1))
                    rows = ROWS[l][t]
                    start, stop = t == 0, last_of(l, t)
                    w = w_at[l, t]
                    if o is None:
                        pe.wait_ge(s_prod, first + pos + 1)
                        for c in range(CH):
                            cols = slice(c * BANK, (c + 1) * BANK)
                            mm = pe.matmul(z[l][:, cols], w_whole[0:rows, w, :],
                                           prod[0:rows, (slot0 + pos) % P_RING, cols], start=start, stop=stop)
                    else:
                        slot = (slot0_s + o) % HALF_RING
                        pe.wait_ge(s_high, first_s + o + 1)
                        for weights in (w_high, w_low):
                            for c in range(CH):
                                cols = slice(c * BANK, (c + 1) * BANK)
                                pe.matmul(z[l][:, cols], weights[0:rows, w, :], high[0:rows, slot, cols],
                                          start=start and weights is w_high, stop=False)
                        pe.wait_ge(s_low, first_s + o + 1)
                        for c in range(CH):
                            cols = slice(c * BANK, (c + 1) * BANK)
                            mm = pe.matmul(z[l][:, cols], w_high[0:rows, w, :], low[0:rows, slot, cols],
                                           start=False, stop=stop)
                    mm.then_inc(s_tile, 1)
                    if kind == "body" and pos in TURN_AT:
                        turn(TURN_AT[pos])

            def mlp_part(part, c0, n):
                done = part * MLP_STEPS
                if part == 0:
                    pe.wait_ge(s_mlpw, 16 * N_MLPW)
                    pe.wait_ge(s_x0t, BT * (D // 4))
                    pe.wait_ge(s_sum2, NB - 1)
                    pe.wait_ge(s_sum01, NB - 1)
                else:
                    pe.wait_ge(s_sum01, NB)
                    pe.wait_ge(s_sum2, NB)

                def free(q):
                    if done + q >= 2:
                        pe.wait_ge(s_mlp_act, done + q - 1)

                for m in range(H1 // P):
                    free(m)
                    ms = slice(m * P, (m + 1) * P)
                    o = spare[m % 2][:, 0:n]
                    pe.matmul(o, wt_dense[:, ms], dense_t[:, c0:c0 + n], start=True, stop=False)
                    pe.matmul(o, wt1[:, 0, ms], sums[:, 0, c0:c0 + n], start=False, stop=False)
                    pe.matmul(o, wt1[:, 1, ms], sums[:, 1, c0:c0 + n], start=False, stop=True).then_inc(s_mlp_mm, 1)
                for m in range(H2 // P):
                    q = H1 // P + m
                    free(q)
                    for c in range(H1 // P):
                        pe.wait_ge(s_mlp_act, done + c + 1)
                        mm = pe.matmul(spare[q % 2][:, 0:n], wt2[:, c, m * P:(m + 1) * P], h1[:, c, 0:n],
                                       start=(c == 0), stop=(c == H1 // P - 1))
                    mm.then_inc(s_mlp_mm, 1)
                q = MLP_STEPS - 1
                free(q)
                for c in range(H2 // P):
                    pe.wait_ge(s_mlp_act, done + H1 // P + c + 1)
                    mm = pe.matmul(spare[q % 2][0:1, 0:n], wt3[:, c:c + 1], h2[:, c, 0:n],
                                   start=(c == 0), stop=(c == H2 // P - 1))
                mm.then_inc(s_mlp_mm, 1)

            tiles("prologue")
            with nc.Fori(0, BT - 1, engines=[mybir.EngineType.PE], hint_back_edge=True) as bt:
                tiles("body", bt)
            tiles("tail", BT - 1)
            mlp_part(1, MAIN, BB)


SUM_AT = {0: 5, 1: 3, 2: 3}
TURN_AT = {7 + 20 + 2 * r: r for r in range(4)}
COPY_LAG = 2
MLP_STEPS = 4 + 2 + 1
N_MLPW = 7
N_WRAW = 4 + 6 + 2 + 5 + 2 + 2


def kernel(**inputs):
    import numpy as _np
    import concourse.bacc as _bacc
    from concourse import mybir as _mybir
    from concourse.bass_utils import run_bass_kernel_spmd as _run

    nc = _bacc.Bacc("TRN2", target_bir_lowering=False, num_devices=1)
    arrays = {}

    def given(name):
        a = _np.ascontiguousarray(inputs[name])
        arrays[f"in_{name}_dram"] = a
        return nc.dram_tensor(f"in_{name}_dram", a.shape, _mybir.dt.from_np(a.dtype), kind="ExternalInput").ap()

    n_tables = inputs["ids"].shape[1]
    out = nc.dram_tensor("out_0_dram", (inputs["ids"].shape[0], 1), _mybir.dt.float32, kind="ExternalOutput").ap()
    cin_tower(nc, given("dense_ctx"), given("ids"), [given(f"tbl_{i}") for i in range(n_tables)],
              given("W_top1"), given("b_top1"), given("W_top2"), given("b_top2"), given("W_top3"),
              [given(f"L0_rec_w{i}") for i in range(3)], [given(f"L0_rec_b{i}") for i in range(3)], out)
    r = _run(nc, [arrays], core_ids=[0])
    return r.results[0]["out_0_dram"]
```

```python
from contextlib import ExitStack

import concourse.bass as bass
from concourse import mybir

F32 = mybir.dt.float32
F32R = mybir.dt.float32r
I32 = mybir.dt.int32
ALU = mybir.AluOpType
ACT = mybir.ActivationFunctionType
AX_X = mybir.AxisListType.X

P = 128
SPLIT = {0: (), 1: ((4, 5), (10, 11), (14, 15)), 2: ((4, 5), (10, 11), (14, 15))}
P_RING, B_RING = 8, 4
AHEAD, REST_AT = 3, 2
LOW, MANY = 10, 21
MID = 4
TURN_AT = {4 + 2 * r: r for r in range(4)}
COPY_LAG = 2
EVACUATE_LAG = {0: 2, 1: 2, 2: 0}
MLP_STEPS = 4 + 2 + 1
N_MLPW = 7
N_WRAW = 4 + 2 * 3


class Group:

    def __init__(self, layer, tiles, block):
        self.layer, self.tiles, self.block, self.slot = layer, tiles, block, None


def cin_tower(nc, dense_ctx, ids, tables, W_top1, b_top1, W_top2, b_top2, W_top3, cin_w, cin_b, out):
    B, DENSE = dense_ctx.shape
    F = len(tables)
    D = tables[0].shape[1]
    S_OUT = cin_w[0].shape[2]
    MAPS = cin_w[1].shape[1]
    H1, H2 = W_top1.shape[1], W_top2.shape[1]

    BANK = 512
    BT = B // P
    BB = P // 2
    NB = B // BB
    COLS = BB * D

    CH = COLS // BANK

    SHIFTS = F // 2 + 1
    SH_PER = P // F
    TILES = {0: -(-SHIFTS // SH_PER), 1: -(-F * MAPS // P), 2: -(-F * MAPS // P)}
    ROWS = {0: [F * SH_PER] * TILES[0]}
    ROWS[1] = ROWS[2] = [min(P, F * MAPS - P * t) for t in range(TILES[1])]
    assert B % P == 0 and MAPS == 64 and S_OUT == P and F % 2 == 1 and D == 16

    small = [f for f in range(F) if tables[f].shape[0] % LOW == 0 and tables[f].shape[0] <= LOW * P][:MANY]
    HIGHS = max(tables[f].shape[0] for f in small) // LOW
    PICKS = BANK // (LOW * D)
    assert len(small) % PICKS == 0
    runs_of_small = [(i, f, next(n for n in range(1, F) if f + n not in small))
                     for i, f in enumerate(small) if f - 1 not in small]

    STACK = TILES[1] - 1
    pairs = [(t, t + 1) for t in range(0, STACK - 1, 2)]
    GROUPS = {0: [tuple(range(t, min(t + 2, TILES[0]))) for t in range(0, TILES[0], 2)]}
    GROUPS[1] = GROUPS[2] = pairs[:MID] + [(STACK - 1, STACK)] + pairs[MID:]
    assert ROWS[1][STACK] == MAPS and STACK % 2 == 1

    def kind(l, t):
        if l and t == STACK:
            return "stack"
        return "split" if any(t in g for g in SPLIT[l]) else "whole"

    def is_split(g):
        return kind(g.layer, g.tiles[0]) == "split"

    def is_cut(g):
        return any(kind(g.layer, t) != "whole" for t in g.tiles)

    def layer(l, block):
        return [Group(l, g, block) for g in GROUPS[l]]

    def half(b):
        two = layer(2, b)
        return two[:REST_AT] + layer(0, b + 1)[AHEAD:] + two[REST_AT:] + with_next(b + 1)

    def with_next(b):
        one, zero = layer(1, b), layer(0, b + 1)
        return one[:-1] + zero[:1] + one[-1:] + zero[1:AHEAD]

    def n_tiles(groups):
        return sum(len(g.tiles) for g in groups)

    def n_cuts(groups):
        return sum(map(is_cut, groups))

    def apart(groups):
        return [Group(groups[0].layer, (t,), groups[0].block) for t in groups[0].tiles] + groups[1:]

    prologue = apart(layer(0, 0)) + apart(with_next(0))
    body = half(0) + half(1)
    tail = [g for g in half(0) if (g.layer, g.block) != (0, 2)] + layer(2, 1)
    HALF = len(half(0))
    assert 2 * HALF % P_RING == 0 and P_RING % 2 == 0
    for groups, ahead in ((prologue, len(body) - len(prologue)), (body, 0), (tail, 0)):
        for n, g in enumerate(groups):
            g.slot = 2 * (n + ahead) % P_RING

    class Run:

        def __init__(self, groups, body_no=None):
            self.groups, self.prologue, self.body_no = groups, body_no is None, body_no
            self.g0 = self.t0 = self.c0 = self.b0 = 0
            if body_no is not None:
                self.g0 = len(prologue) + body_no * len(body)
                self.t0 = n_tiles(prologue) + body_no * n_tiles(body)
                self.c0 = n_cuts(prologue) + body_no * n_cuts(body)
                self.b0 = body_no * 2

        def find(self, l, block):
            return [n for n, g in enumerate(self.groups) if (g.layer, g.block) == (l, block)]

        def block(self, n):
            return self.b0 + self.groups[n].block

        def products(self, n):
            return self.g0 + n + 1

        def tiles(self, n, k=0):
            if n < 0:
                return self.t0 - n_tiles(body[len(body) + n + 1:]) - (len(body[n].tiles) - 1 - k)
            return self.t0 + n_tiles(self.groups[:n]) + k + 1

        def cuts(self, n):
            return self.c0 + (n_cuts(self.groups[:n + 1]) if n >= 0 else -n_cuts(body[len(body) + n + 1:]))

        def back(self, n, fits):
            for m in range(n - 1, -1 if self.prologue else -len(pairs) - 1, -1):
                g = self.groups[m] if m >= 0 else body[m]
                for k in reversed(range(len(g.tiles))):
                    if fits(g, k):
                        return m, k
            return None

        def same(self, m):
            return self.groups[m] if m >= 0 else body[m]

    w_at, n_of = {}, {"whole": 0, "split": 0, "stack": 0}
    for l in range(3):
        for t in range(TILES[l]):
            w_at[l, t] = n_of[kind(l, t)]
            n_of[kind(l, t)] += 1

    def tiles_of(what):
        return [(l, t) for l in range(3) for t in range(TILES[l]) if kind(l, t) == what]

    with ExitStack() as ctx:
        def sb(name, shape, dt=F32):
            return ctx.enter_context(nc.sbuf_tensor(name, shape, dt))

        def psum(name, shape):
            return ctx.enter_context(nc.psum_tensor(name, shape, F32))

        def sem(name):
            return ctx.enter_context(nc.semaphore(name))

        x0rep = sb("x0rep", [P, TILES[1], COLS])
        staged = x0rep[:].rearrange("p t c -> p (t c)")
        w_whole = sb("w_whole", [P, n_of["whole"], S_OUT])
        w_high = sb("w_high", [P, n_of["split"], S_OUT], F32R)
        w_low = sb("w_low", [P, n_of["split"], S_OUT], F32R)
        w_stack = sb("w_stack", [P, n_of["stack"], S_OUT], F32R)
        w_stack_low = sb("w_stack_low", [MAPS, n_of["stack"], S_OUT], F32R)
        prod = sb("prod", [P, P_RING, COLS])
        high = sb("high", [P, 2, COLS], F32R)
        low = sb("low", [P, 2, COLS], F32R)
        stack = low[:, 0, :]
        xk = {1: sb("xk1", [P, COLS]), 2: sb("xk2", [P, COLS])}
        x0a = sb("x0a", [P, COLS])
        x0b = sb("x0b", [P, B_RING, COLS])
        direct01 = sb("direct01", [P, COLS])
        emb = sb("emb", [P, F, D])
        turned = sb("turned", [P, 2 * D * BB])
        x0t = turned[0:F, :].rearrange("p (i d b) -> p i d b", i=2, d=D)
        dense_t = turned[MAPS:MAPS + DENSE, 0:B]
        wt_dense = turned[MAPS:MAPS + DENSE, B:B + H1]
        ids_sb = sb("ids_sb", [P, BT, F], I32)
        ident = sb("ident", [P, P])
        last_sum = sb("last_sum", [P, BB])
        sums = sb("sums", [P, 2, B])
        dense_sb = sb("dense_sb", [P, BT, DENSE])
        wt3 = sb("wt3", [P, H2 // P])
        bias = sb("bias", [P, 3 + H1 // P + H2 // P])
        MAIN = B - BB
        y_sb = emb[0:1].rearrange("p f d -> p (f d)")[:, 0:B]
        wt2 = x0a[:].rearrange("p (c m) -> p c m", m=H2)
        mlp = x0b[:].rearrange("p r c -> p (r c)")
        h1 = mlp[:, 0:H1 // P * MAIN].rearrange("p (m n) -> p m n", n=MAIN)
        h2 = mlp[:, H1 // P * MAIN:(H1 + H2) // P * MAIN].rearrange("p (m n) -> p m n", n=MAIN)
        wt1 = mlp[:, B_RING * COLS - 2 * H1:].rearrange("p (c m) -> p c m", m=H1)
        assert H1 // P * H2 == COLS and (H1 + H2) // P * MAIN + 2 * H1 <= B_RING * COLS

        N_S = len(small)

        def room(sizes, start):
            for size in sizes:
                yield staged[:, start:start + size]
                start += size
            assert start <= STACK * COLS

        parts = room((N_S * LOW * D, N_S * (HIGHS + 1), N_S * HIGHS, N_S * LOW, N_S, N_S, N_S, N_S * P),
                     2 * (TILES[0] + TILES[1]) * S_OUT)
        small_tables = next(parts).rearrange("p (f c) -> p f c", c=LOW * D)
        reached = next(parts).rearrange("p (f j) -> p f j", j=HIGHS + 1)
        is_high = next(parts).rearrange("p (f j) -> p f j", j=HIGHS)
        is_low = next(parts).rearrange("p (f j) -> p f j", j=LOW)
        small_ids, highs, lows = next(parts), next(parts), next(parts)
        high_t = next(parts)[0:HIGHS, :].rearrange("p (f b) -> p f b", b=P)
        picked = x0b[:].rearrange("p r c -> p (r c)")[:, 0:2 * PICKS * LOW * D].rearrange(
            "p (i f l d) -> p i f l d", i=2, f=PICKS, d=D)
        steps = x0a[:, 0:HIGHS + 1]
        lows_all = x0a[:, HIGHS + 1:HIGHS + 1 + LOW]

        z = [psum(f"z{l}", [P, COLS]) for l in range(3)]
        spare = [psum(f"spare{i}", [P, BANK]) for i in range(2)]

        w0_cols = nc.dram_tensor("w0_cols", (F, F + SHIFTS, S_OUT), F32, kind="Internal").ap()
        w0_rows = nc.dram_tensor("w0_rows", (F + SHIFTS, F, S_OUT), F32, kind="Internal").ap()
        x0_dram = nc.dram_tensor("x0_dram", (NB, 2 * F, COLS), F32, kind="Internal").ap()

        s_ids = sem("ids_loaded")
        s_dense = sem("dense_loaded")
        s_wdram = sem("w0_copied")
        s_wraw = sem("cin_weights_loaded")
        s_zero = sem("staging_zeroed")
        s_mlpw = sem("mlp_weights_loaded")
        s_bias = sem("biases_loaded")
        s_ident = sem("identity_made")
        s_iota = sem("row_number_steps_made")
        s_tables = [sem(f"small_tables{i}_loaded") for i in range(N_S // PICKS)]
        s_ids_cast = sem("small_ids_cast")
        s_numbers = sem("row_numbers_cut")
        s_high_turned = sem("high_indicators_transposed")
        s_high_copied = sem("high_indicators_copied")
        s_candidates = sem("candidates_made")
        s_picked = sem("candidates_masked")
        s_found = sem("small_rows_found")
        s_wsum = sem("pair_weights_added")
        s_wcopy = sem("whole_weights_copied")
        s_whigh = sem("high_weights_made")
        s_wlow = sem("low_weights_made")
        s_gather = sem("rows_gathered")
        s_turned = sem("transposes_done")
        s_x0t = sem("x0t_copied")
        s_dram = sem("x0_written")
        s_x0a = sem("x0a_loaded")
        s_x0b = [sem(f"x0b{i}_loaded") for i in range(B_RING)]
        s_x0rep = [sem(f"x0rep{t}_loaded") for t in range(TILES[1])]
        s_prod = sem("products_done")
        s_high = sem("highs_done")
        s_low = sem("lows_done")
        s_tile = sem("tiles_contracted")
        s_bank = [sem(f"z{l}_first_bank_complete") for l in range(3)]
        s_xk = {1: sem("xk1_ready"), 2: sem("xk2_ready")}
        s_read = [sem(f"z{l}_evacuated") for l in range(3)]
        s_sum01 = sem("direct01_summed")
        s_sum2 = sem("direct2_summed")
        s_dense_turned = sem("dense_transposed")
        s_dense_copied = sem("dense_copied")
        s_mlp_mm = sem("mlp_matmuls_done")
        s_mlp_act = sem("mlp_activated")
        s_out = sem("out_written")

        def block_rows(b):
            if isinstance(b, int):
                return x0_dram[b]
            return x0_dram[bass.ds(b, 1), :, :].rearrange("o r c -> (o r) c")

        MLP_BANKS = [spare[q % 2] for q in range(MLP_STEPS)]
        LAST_BANKS = [z[m // 2][:, m % 2 * BANK:(m % 2 + 1) * BANK] for m in range(H1 // P)] + spare
        LAST_BANKS.append(LAST_BANKS[0])
        assert H1 // P == 4 and H2 // P == 2

        def candidates(i):
            return z[0][:, i % 2 * BANK:(i % 2 + 1) * BANK]

        per_bank = [slice(i, min(i + BANK // P, N_S)) for i in range(0, N_S, BANK // P)]

        def high_bank(i):
            return z[1 + i // 2][:, i % 2 * BANK:(i % 2 + 1) * BANK] if i < 4 else spare[i % 4]

        def first_turns():
            banks = iter([spare[0], z[2][:, 0:BANK], z[1][:, 0:BANK], z[1][:, BANK:2 * BANK]])
            for i in range(2):
                for d in range(0, D, BANK // BB):
                    yield i, slice(d, d + BANK // BB), next(banks)

        RAW = {1: 0, 2: TILES[1] * S_OUT, 0: 2 * TILES[1] * S_OUT}
        RAW_T = RAW[0] + TILES[0] * S_OUT

        def raw(l, t, rows):
            return staged[0:rows, RAW[l] + t * S_OUT:RAW[l] + (t + 1) * S_OUT]

        N_WHOLE, N_HIGH, N_LOW = n_of["whole"], n_of["split"] + 2 * n_of["stack"], n_of["split"] + n_of["stack"]

        blk = ctx.enter_context(nc.Block())

        def load_tables(queue, parity):
            for i, f in enumerate(small):
                if i % 2 == parity:
                    queue.dma_start(small_tables[0:tables[f].shape[0] // LOW, i, :],
                                    tables[f].rearrange("(h l) d -> h (l d)", l=LOW)
                                    ).then_inc(s_tables[i // PICKS], 16)

        @blk.sync
        def _(sp):
            sp.dma_start(ids_sb[:], ids.rearrange("(t p) f -> p t f", p=P)).then_inc(s_ids, 16)
            load_tables(sp, 0)
            sp.dma_start(dense_sb[:], dense_ctx.rearrange("(t p) f -> p t f", p=P)).then_inc(s_dense, 16)
            full = F * MAPS // P
            for l in (1, 2):
                flat = cin_w[l].rearrange("h k s -> (h k) s")
                dst = staged[:, RAW[l]:RAW[l] + full * S_OUT].rearrange("p (t s) -> p t s", s=S_OUT)
                sp.dma_start(dst, flat[0:full * P, :].rearrange("(t p) s -> p t s", p=P)).then_inc(s_wraw, 16)
                sp.dma_start(raw(l, full, F * MAPS - full * P), flat[full * P:, :]).then_inc(s_wraw, 16)

            sp.wait_ge(s_wdram, 4 * 16)
            sp.wait_ge(s_zero, 1)

            def load_w0(j, tiles, at, src, per_h, per_k):
                n = len(tiles)
                sp.dma_start(staged[j:F * SH_PER:SH_PER, at + tiles[0] * S_OUT:at + (tiles[-1] + 1) * S_OUT
                                     ].rearrange("p (t s) -> p t s", s=S_OUT),
                              bass.AP(src.tensor, (SH_PER * tiles[0] + j) * per_k,
                                      [[per_h + per_k, F], [SH_PER * per_k, n], [1, S_OUT]])).then_inc(s_wraw, 16)

            for j in range(SH_PER):
                tiles = [t for t in range(TILES[0]) if SH_PER * t + j < SHIFTS]
                load_w0(j, tiles, RAW[0], w0_cols, (F + SHIFTS) * S_OUT, S_OUT)
                load_w0(j, [t for t in tiles if t or j], RAW_T, w0_rows, S_OUT, F * S_OUT)

            def overlapped(b, row, step):
                rows = block_rows(b)[row:row + F, :]
                return bass.AP(rows.tensor, rows.offset, [[COLS, F], [step * COLS, SH_PER], [1, COLS]])

            def load_x0a(b):
                sp.dma_start(x0a[0:F * SH_PER, :], overlapped(b, F, 0)).then_inc(s_x0a, 16)

            def load_x0b(b, t):
                sp.dma_start(x0b[0:F * SH_PER, t % B_RING, :], overlapped(b, SH_PER * t, 1)
                             ).then_inc(s_x0b[t % B_RING], 16)

            def load_x0rep(b, t):
                for j in range(ROWS[1][t] // MAPS):
                    h = 2 * t + j or F
                    row = block_rows(b)[h:h + 1, :]
                    sp.dma_start(x0rep[j * MAPS:(j + 1) * MAPS, t, :],
                                 row.broadcast_to((MAPS, COLS))).then_inc(s_x0rep[t], 16)

            def heads(b):
                load_x0a(b)
                for t in range(B_RING):
                    load_x0b(b, t)

            def rest_of_x0b(b, run, block):
                for n in run.find(0, block):
                    tiles = [t + B_RING for t in run.groups[n].tiles if t + B_RING < TILES[0]]
                    if tiles:
                        sp.wait_ge(s_prod, run.products(n))
                    for t in tiles:
                        load_x0b(b, t)

            def write_block(bt, i, rounds):
                sp.wait_ge(s_x0t, rounds)
                for twice in (1, 0):
                    sp.dma_start(block_rows(bt * 2 + i)[twice * F:(twice + 1) * F, :],
                                 x0t[:, i].rearrange("p d b -> p (d b)")).then_inc(s_dram, 16)

            def write_x0(bt, rounds):
                for i in range(2):
                    write_block(bt, i, rounds)

            write_block(0, 0, 2)
            sp.wait_ge(s_dram, 2 * 16)
            heads(0)
            write_block(0, 1, 4)
            rest_of_x0b(0, Run(prologue), 0)
            sp.wait_ge(s_wcopy, N_WHOLE)
            sp.wait_ge(s_whigh, N_HIGH)
            sp.wait_ge(s_wlow, N_LOW)
            run = Run(prologue)
            for g in GROUPS[1]:
                if g == GROUPS[1][-1]:
                    sp.wait_ge(s_prod, run.products(run.find(0, 0)[-1]))
                    sp.wait_ge(s_dram, 4 * 16)
                    heads(1)
                for t in g:
                    load_x0rep(0, t)
            rest_of_x0b(1, run, 1)

            def one_half(run, i, turned):
                b = run.b0 + i
                for n, g in zip(run.find(2, i), GROUPS[2]):
                    sp.wait_ge(s_prod, run.products(n))
                    for t in g:
                        load_x0rep(b + 1, t)
                if turned is not None:
                    write_x0(turned, (turned + 1) * (D // 4))
                    sp.wait_ge(s_dram, (turned + 1) * 64)

            with nc.Fori(0, BT - 1, engines=[mybir.EngineType.SP], hint_back_edge=True) as bt:
                run = Run(body, bt)
                one_half(run, 0, bt + 1)
                heads(bt * 2 + 2)
                rest_of_x0b(bt * 2 + 2, run, 2)
                one_half(run, 1, None)
                heads(bt * 2 + 3)
                rest_of_x0b(bt * 2 + 3, run, 3)
            run = Run(tail, BT - 1)
            one_half(run, 0, None)
            sp.wait_ge(s_prod, run.products(run.find(0, 1)[-1]))
            direct = P - MAPS
            sp.dma_start(wt1[0:direct, 0, :], W_top1[direct:2 * direct, :]).then_inc(s_mlpw, 16)
            sp.dma_start(wt1[direct:P, 0, :], W_top1[0:direct, :]).then_inc(s_mlpw, 16)
            sp.dma_start(wt1[:, 1, :], W_top1[P:2 * P, :]).then_inc(s_mlpw, 16)
            sp.dma_start(wt2[:], W_top2.rearrange("(c p) m -> p c m", p=P)).then_inc(s_mlpw, 16)
            sp.wait_ge(s_mlp_act, 2 * (H1 // P + H2 // P + 1))
            sp.dma_start(out.rearrange("b o -> o b"), y_sb[:]).then_inc(s_out, 16)
            sp.wait_ge(s_out, 16)

        @blk.gpsimd
        def _(pool):
            pool.memset(ident[:], 0.0).then_inc(s_ident, 1)
            pool.wait_ge(s_ident, 1)
            pool.affine_select(out=ident[:], in_=ident[:], compare_op=ALU.not_equal, fill=1.0,
                               base=0, pattern=[[-1, P]], channel_multiplier=1).then_inc(s_ident, 1)
            pool.iota(steps, [[LOW, HIGHS + 1]], base=0, channel_multiplier=0,
                      allow_small_or_imprecise_dtypes=True).then_inc(s_iota, 1)
            pool.iota(lows_all, [[1, LOW]], base=0, channel_multiplier=0,
                      allow_small_or_imprecise_dtypes=True).then_inc(s_iota, 1)
            pool.wait_ge(s_ids, 16)

            def gather(t, column):
                for f in range(F):
                    if t == 0 and f in small:
                        continue
                    pool.indirect_dma_start(
                        emb[:, f, :], None, tables[f],
                        bass.IndirectOffsetOnAxis(ap=column(f), axis=0)).then_inc(s_gather, 16)

            for t in range(BT):
                if t:
                    pool.wait_ge(s_turned, t * D // 4)
                gather(t, lambda f: ids_sb[:, t, f:f + 1])

        @blk.scalar
        def _(act):
            load_tables(act, 1)
            act.dma_start(w0_cols[:, 0:F, :], cin_w[0]).then_inc(s_wdram, 16)
            act.dma_start(w0_cols[:, F:, :], cin_w[0][:, 0:SHIFTS, :]).then_inc(s_wdram, 16)
            act.dma_start(w0_rows[0:F], cin_w[0]).then_inc(s_wdram, 16)
            act.dma_start(w0_rows[F:], cin_w[0][0:SHIFTS]).then_inc(s_wdram, 16)

            def copy_x0t(r, before):
                act.wait_ge(s_turned, before + r + 1)
                act.activation(x0t[:, :, 4 * r:4 * r + 4, :].rearrange("p i d b -> p d i b"),
                               spare[r % 2][0:F, :].rearrange("p (d i b) -> p d i b", d=4, i=2),
                               ACT.Copy).then_inc(s_x0t, 1)

            act.wait_ge(s_dense_turned, 1)
            act.activation(dense_t, spare[1][0:DENSE, 0:B], ACT.Copy).then_inc(s_dense_copied, 1)

            for r, (i, dims, bank) in enumerate(first_turns()):
                act.wait_ge(s_turned, r + 1)
                act.activation(x0t[:, i, dims, :], bank[0:F, :].rearrange("p (d b) -> p d b", b=BB), ACT.Copy
                               ).then_inc(s_x0t, 1)

            act.wait_ge(s_wraw, 16 * N_WRAW)
            act.wait_ge(s_wsum, 1)
            for l, t in tiles_of("split"):
                r = ROWS[l][t]
                act.activation(w_high[0:r, w_at[l, t], :], raw(l, t, r), ACT.Copy).then_inc(s_whigh, 1)
            for l, t in tiles_of("stack"):
                for half_rows in (slice(0, MAPS), slice(MAPS, P)):
                    act.activation(w_stack[half_rows, w_at[l, t], :], raw(l, t, MAPS), ACT.Copy
                                   ).then_inc(s_whigh, 1)

            act.wait_ge(s_prod, 1)
            for l in range(3):
                act.dma_start(bias[:, l:l + 1], cin_b[l].rearrange("(p o) -> p o", o=1)).then_inc(s_bias, 16)
            for m in range(H1 // P):
                act.dma_start(bias[:, 3 + m:4 + m],
                              b_top1[m * P:(m + 1) * P].rearrange("(p o) -> p o", o=1)).then_inc(s_bias, 16)
            for m in range(H2 // P):
                act.dma_start(bias[:, 3 + H1 // P + m:4 + H1 // P + m],
                              b_top2[m * P:(m + 1) * P].rearrange("(p o) -> p o", o=1)).then_inc(s_bias, 16)
            act.dma_start(wt_dense, W_top1[2 * P:2 * P + DENSE, :]).then_inc(s_mlpw, 16)
            for c in range(H2 // P):
                act.dma_start(wt3[:, c:c + 1], W_top3[c * P:(c + 1) * P, :]).then_inc(s_mlpw, 16)

            act.wait_ge(s_bias, 16 * (3 + H1 // P + H2 // P))

            def evacuate(l, tiles, b):
                maps, rest = slice(0, MAPS), slice(MAPS, P)

                def relu(dst, rows, c):
                    cols = slice(c * BANK, (c + 1) * BANK)
                    return act.activation(dst[:, cols], z[l][rows, cols], ACT.Relu, bias=bias[rows, l:l + 1])

                for c in range(CH):
                    if c == 0:
                        act.wait_ge(s_bank[l], b + 1)
                    else:
                        act.wait_ge(s_tile, tiles)
                    if l == 2:
                        relu(z[2], slice(0, P), c).then_inc(s_read[2], 1)
                    else:
                        relu(xk[l + 1][maps, :], maps, c)
                        mm = relu(xk[l + 1][rest, :], maps, c)
                if l == 2:
                    return
                mm.then_inc(s_xk[l + 1], 1)
                if not isinstance(b, int) or b:
                    act.wait_ge(s_sum01, b)
                for c in range(CH):
                    mm = relu(direct01[rest if l == 0 else maps, :], rest, c)
                mm.then_inc(s_read[l], 1)

            def groups(run, turn_at, mlp_at=None):
                def at_once(m):
                    return run.prologue and run.groups[m].layer == 0 or m + 1 == mlp_at

                for n, g in enumerate(run.groups):
                    l = g.layer
                    if n == mlp_at:
                        mlp_part(0, MAIN, MLP_BANKS)
                    if is_cut(g):
                        act.wait_ge(s_prod, run.products(n))
                        user = run.back(n, lambda u, k: is_cut(u) and k == len(u.tiles) - 1)
                        if user:
                            act.wait_ge(s_tile, run.tiles(*user))
                        if is_split(g):
                            rows = ROWS[l][g.tiles[0]]
                            act.activation(high[0:rows], prod[0:rows, g.slot:g.slot + 2, :], ACT.Copy
                                           ).then_inc(s_high, 1)
                        else:
                            act.activation(stack[0:MAPS, :], prod[0:MAPS, g.slot + 1, :], ACT.Copy
                                           ).then_inc(s_high, 1)
                    for m, h in enumerate(run.groups[:n + 1]):
                        lag = 0 if at_once(m) else EVACUATE_LAG[h.layer]
                        if h.tiles == GROUPS[h.layer][-1] and n == min(m + lag, len(run.groups) - 1):
                            evacuate(h.layer, run.tiles(m, len(h.tiles) - 1), run.block(m))
                    if n - COPY_LAG in turn_at:
                        r = turn_at[n - COPY_LAG]
                        before = run.body_no + 1
                        if r == 0:
                            act.wait_ge(s_dram, before * 64)
                        copy_x0t(r, before * (D // 4))

            def mlp_part(part, n, banks):
                done = part * MLP_STEPS
                for q, bank in enumerate(banks):
                    act.wait_ge(s_mlp_mm, done + q + 1)
                    if q < H1 // P:
                        act.activation(h1[:, q, 0:n], bank[:, 0:n], ACT.Relu, bias=bias[:, 3 + q:4 + q]
                                       ).then_inc(s_mlp_act, 1)
                    elif q < MLP_STEPS - 1:
                        act.activation(h2[:, q - H1 // P, 0:n], bank[:, 0:n], ACT.Relu, bias=bias[:, 3 + q:4 + q]
                                       ).then_inc(s_mlp_act, 1)
                    else:
                        c0 = part * MAIN
                        act.activation(y_sb[:, c0:c0 + n], bank[0:1, 0:n], ACT.Copy).then_inc(s_mlp_act, 1)

            groups(Run(prologue), {})
            with nc.Fori(0, BT - 1, engines=[mybir.EngineType.Activation], hint_back_edge=True) as bt:
                groups(Run(body, bt), TURN_AT)
            groups(Run(tail, BT - 1), {}, mlp_at=HALF - AHEAD)
            mlp_part(1, BB, LAST_BANKS)

        @blk.vector
        def _(dve):
            dve.memset(staged[:, RAW[0]:RAW_T + TILES[0] * S_OUT], 0.0).then_inc(s_zero, 1)
            dve.memset(x0rep[MAPS:P, STACK, :], 0.0).then_inc(s_zero, 1)
            assert RAW_T + TILES[0] * S_OUT <= STACK * COLS
            dve.wait_ge(s_ids, 16)
            for i, f, n in runs_of_small:
                dve.tensor_copy(small_ids[:, i:i + n], ids_sb[:, 0, f:f + n]).then_inc(s_ids_cast, 1)
            dve.wait_ge(s_ids_cast, len(runs_of_small))
            dve.wait_ge(s_iota, 2)
            dve.tensor_tensor(reached, small_ids.unsqueeze(2).broadcast_to((P, N_S, HIGHS + 1)),
                              steps.unsqueeze(1).broadcast_to((P, N_S, HIGHS + 1)), ALU.is_ge
                              ).then_inc(s_numbers, 1)
            dve.wait_ge(s_numbers, 1)
            dve.tensor_tensor(is_high, reached[:, :, 0:HIGHS], reached[:, :, 1:HIGHS + 1], ALU.subtract
                              ).then_inc(s_numbers, 1)
            dve.tensor_reduce(highs, reached[:, :, 1:HIGHS + 1], AX_X, ALU.add).then_inc(s_numbers, 1)
            dve.wait_ge(s_numbers, 3)
            dve.tensor_scalar(lows, highs, -float(LOW), None, ALU.mult).then_inc(s_numbers, 1)
            dve.wait_ge(s_numbers, 4)
            dve.tensor_tensor(highs, lows, small_ids, ALU.add).then_inc(s_numbers, 1)
            dve.wait_ge(s_numbers, 5)
            dve.tensor_tensor(is_low, highs.unsqueeze(2).broadcast_to((P, N_S, LOW)),
                              lows_all.unsqueeze(1).broadcast_to((P, N_S, LOW)), ALU.is_equal
                              ).then_inc(s_numbers, 1)
            dve.wait_ge(s_numbers, 6)

            for i, part in enumerate(per_bank):
                dve.wait_ge(s_high_turned, i + 1)
                bank = high_bank(i)[0:HIGHS, 0:(part.stop - part.start) * P]
                dve.tensor_copy(high_t[:, part, :], bank.rearrange("p (f b) -> p f b", b=P)
                                ).then_inc(s_high_copied, 1)

            def pick(i):
                dve.wait_ge(s_candidates, i + 1)
                if i >= 2:
                    dve.wait_ge(s_found, (i - 1) * PICKS)
                dve.tensor_tensor(picked[:, i % 2],
                                  candidates(i)[:, 0:PICKS * LOW * D].rearrange("p (f l d) -> p f l d", l=LOW, d=D),
                                  is_low[:, i * PICKS:(i + 1) * PICKS, :].unsqueeze(3).broadcast_to(
                                      (P, PICKS, LOW, D)), ALU.mult).then_inc(s_picked, 1)

            def find(i):
                dve.wait_ge(s_picked, i + 1)
                for j in range(PICKS):
                    dve.tensor_reduce(emb[:, small[i * PICKS + j], :], picked[:, i % 2, j].rearrange("p l d -> p d l"),
                                      AX_X, ALU.add).then_inc(s_found, 1)

            for i in range(N_S // PICKS):
                pick(i)
                if i:
                    find(i - 1)
            find(N_S // PICKS - 1)
            dve.wait_ge(s_wraw, 16 * N_WRAW)
            n = TILES[0] * S_OUT
            dve.tensor_tensor(staged[:, RAW[0]:RAW[0] + n], staged[:, RAW[0]:RAW[0] + n],
                              staged[:, RAW_T:RAW_T + n], ALU.add).then_inc(s_wsum, 1)
            dve.wait_ge(s_wsum, 1)
            for l, t in tiles_of("whole"):
                r = ROWS[l][t]
                dve.tensor_copy(w_whole[0:r, w_at[l, t], :], raw(l, t, r)).then_inc(s_wcopy, 1)

            def low_weights():
                dve.wait_ge(s_whigh, N_HIGH)
                for l, t in tiles_of("split"):
                    r = ROWS[l][t]
                    dve.tensor_tensor(w_low[0:r, w_at[l, t], :], raw(l, t, r),
                                      w_high[0:r, w_at[l, t], :].bitcast(F32), ALU.subtract).then_inc(s_wlow, 1)
                for l, t in tiles_of("stack"):
                    dve.tensor_tensor(w_stack_low[:, w_at[l, t], :], raw(l, t, MAPS),
                                      w_stack[0:MAPS, w_at[l, t], :].bitcast(F32), ALU.subtract).then_inc(s_wlow, 1)

            def sum01(b):
                dve.wait_ge(s_read[1], b + 1)
                dve.wait_ge(s_read[0], b + 1)
                dve.tensor_reduce(columns(0, b), direct01[:].rearrange("p (d b) -> p b d", d=D),
                                  AX_X, ALU.add).then_inc(s_sum01, 1)

            def sum2(b):
                dve.wait_ge(s_read[2], (b + 1) * CH)
                dve.tensor_reduce(columns(1, b), z[2][:].rearrange("p (d b) -> p b d", d=D),
                                  AX_X, ALU.add).then_inc(s_sum2, 1)

            def last_sum2(b):
                for c, dst in enumerate((columns(1, b), last_sum[:])):
                    dve.wait_ge(s_read[2], b * CH + c + 1)
                    dve.tensor_reduce(dst, z[2][:, c * BANK:(c + 1) * BANK].rearrange("p (d b) -> p b d", b=BB),
                                      AX_X, ALU.add).then_inc(s_sum2, 1)

            def columns(part, b):
                return sums[:, part, slice(b * BB, (b + 1) * BB) if isinstance(b, int) else bass.ds(b * BB, BB)]

            def low_part(run, n):
                g = run.same(n)
                rows = ROWS[g.layer][g.tiles[0]]
                dve.wait_ge(s_high, run.cuts(n))
                if is_split(g):
                    dve.tensor_tensor(low[0:rows], prod[0:rows, g.slot:g.slot + 2, :],
                                      high[0:rows].bitcast(F32), ALU.subtract).then_inc(s_low, 1)
                else:
                    dve.tensor_tensor(stack[MAPS:P, :], prod[0:MAPS, g.slot + 1, :],
                                      stack[0:MAPS, :].bitcast(F32), ALU.subtract).then_inc(s_low, 1)

            def groups(run):
                for n, g in enumerate(run.groups):
                    l, b, size = g.layer, run.block(n), len(g.tiles)
                    rows = ROWS[l][g.tiles[0]]
                    dst = prod[0:rows, g.slot:g.slot + size, :]
                    users = [u for u in (run.back(n, lambda h, k: h.slot + k == g.slot + i)
                                         for i in range(size)) if u]
                    whole = [u for u in users if kind(run.same(u[0]).layer, run.same(u[0]).tiles[u[1]]) == "whole"]
                    if whole:
                        dve.wait_ge(s_tile, run.tiles(*max(whole)))
                    if len(users) > len(whole):
                        dve.wait_ge(s_low, run.cuts(max(u for u in users if u not in whole)[0]))
                    first = g.tiles[0] == 0
                    if l == 0:
                        if first:
                            dve.wait_ge(s_x0a, (b + 1) * 16)
                        for t in g.tiles:
                            loads = len(range(t % B_RING, TILES[0], B_RING))
                            dve.wait_ge(s_x0b[t % B_RING], (b * loads + t // B_RING + 1) * 16)
                        at = g.tiles[0] % B_RING
                        in0 = x0b[0:rows, at:at + size, :]
                        in1 = x0a[0:rows, :]
                    else:
                        if first:
                            dve.wait_ge(s_xk[l], b + 1)
                        if l == 1:
                            for t in g.tiles:
                                dve.wait_ge(s_x0rep[t], (b + 1) * 16 * (ROWS[l][t] // MAPS))
                        in0 = x0rep[:, g.tiles[0]:g.tiles[0] + size, :]
                        in1 = xk[l][:]
                    in1 = in1.unsqueeze(1).broadcast_to((rows, size, COLS))
                    dve.tensor_tensor(dst, in0, in1, ALU.mult).then_inc(s_prod, 1)
                    if run.prologue and n == 1:
                        low_weights()
                    if (n or not run.prologue) and is_cut(run.same(n - 1)):
                        low_part(run, n - 1)
                    if not run.prologue and l == 2 and g.tiles == GROUPS[l][0]:
                        sum01(b)
                    if n + 1 == len(run.groups):
                        if run.groups is body:
                            sum2(run.b0 + 1)
                    elif (run.groups[n + 1].layer, run.groups[n + 1].tiles) == (2, GROUPS[2][0]):
                        sum2(run.block(n + 1) - 1)

            groups(Run(prologue))
            with nc.Fori(0, BT - 1, engines=[mybir.EngineType.DVE], hint_back_edge=True) as bt:
                groups(Run(body, bt))
            groups(Run(tail, BT - 1))
            last_sum2(NB - 1)

        @blk.tensor
        def _(pe):
            pe.wait_ge(s_ident, 2)
            pe.wait_ge(s_numbers, 2)
            for i, part in enumerate(per_bank):
                for j, f in enumerate(range(N_S)[part]):
                    mm = pe.transpose(high_bank(i)[0:HIGHS, j * P:(j + 1) * P], is_high[:, f, :], ident[:])
                mm.then_inc(s_high_turned, 1)
            for i in range(N_S):
                pe.wait_ge(s_high_copied, i // (BANK // P) + 1)
                bank, at = divmod(i, PICKS)
                if at == 0:
                    pe.wait_ge(s_tables[bank], 16 * PICKS)
                if at == 0 and bank >= 2:
                    pe.wait_ge(s_picked, bank - 1)
                rows = tables[small[i]].shape[0] // LOW
                mm = pe.matmul(candidates(bank)[:, at * LOW * D:(at + 1) * LOW * D], high_t[0:rows, i, :],
                               small_tables[0:rows, i, :], start=True, stop=True)
                if at == PICKS - 1:
                    mm.then_inc(s_candidates, 1)
            pe.wait_ge(s_dense, 16)
            for t in range(BT):
                mm = pe.transpose(spare[1][0:DENSE, t * P:(t + 1) * P], dense_sb[:, t, :], ident[:])
            mm.then_inc(s_dense_turned, 1)

            def turn(r):
                for i in range(4):
                    mm = pe.transpose(spare[r % 2][0:F, i * P:(i + 1) * P], emb[:, :, 4 * r + i], ident[:])
                mm.then_inc(s_turned, 1)

            pe.wait_ge(s_gather, 16 * (F - N_S))
            pe.wait_ge(s_found, N_S)
            for i, dims, bank in first_turns():
                rows = slice(i * BB, (i + 1) * BB)
                for j, d in enumerate(range(D)[dims]):
                    mm = pe.transpose(bank[0:F, j * BB:(j + 1) * BB], emb[rows, :, d], ident[rows, rows])
                mm.then_inc(s_turned, 1)
            pe.wait_ge(s_wcopy, N_WHOLE)
            pe.wait_ge(s_x0t, D // 4)
            pe.wait_ge(s_dense_copied, 1)

            def contract(l, weights, data, start, stop, banks=range(CH)):
                for c in banks:
                    cols = slice(c * BANK, (c + 1) * BANK)
                    mm = pe.matmul(z[l][:, cols], weights, data[:, cols], start=start, stop=stop)
                return mm

            def complete(run, n):
                g = run.groups[n]
                l = g.layer
                for c in range(CH):
                    for k, t in enumerate(g.tiles):
                        mm = contract(l, w_whole[0:ROWS[l][t], w_at[l, t], :],
                                      prod[0:ROWS[l][t], g.slot + k, :], False, t == g.tiles[-1], [c])
                    mm.then_inc(s_tile, len(g.tiles)) if c else mm.then_inc(s_bank[l], 1)

            def add(run, n):
                g = run.groups[n]
                l = g.layer
                for k, t in enumerate(g.tiles):
                    r, w, what = ROWS[l][t], w_at[l, t], kind(l, t)
                    start = t == GROUPS[l][0][0]
                    if what == "whole":
                        mm = contract(l, w_whole[0:r, w, :], prod[0:r, g.slot + k, :], start, False)
                    elif what == "stack":
                        pe.wait_ge(s_high, run.cuts(n))
                        contract(l, w_stack_low[:, w, :], stack[0:r, :], False, False)
                        pe.wait_ge(s_low, run.cuts(n))
                        mm = contract(l, w_stack[:, w, :], stack, False, False)
                    else:
                        if k == 0:
                            pe.wait_ge(s_high, run.cuts(n))
                            for j, u in enumerate(g.tiles):
                                contract(l, w_high[0:r, w_at[l, u], :], high[0:r, j, :], False, False)
                                contract(l, w_low[0:r, w_at[l, u], :], high[0:r, j, :], False, False)
                            pe.wait_ge(s_low, run.cuts(n))
                        mm = contract(l, w_high[0:r, w, :], low[0:r, k, :], False, False)
                    mm.then_inc(s_tile, 1)

            def groups(run, turn_at, mlp_at=None):
                for n, g in enumerate(run.groups):
                    l, b = g.layer, run.block(n)
                    if n == mlp_at:
                        mlp_main()
                    if run.prologue and is_cut(g):
                        pe.wait_ge(s_whigh, N_HIGH)
                        pe.wait_ge(s_wlow, N_LOW)
                    if mlp_at is not None and n + 1 == len(run.groups):
                        mlp_ahead()
                    if g.tiles[0] == 0:
                        if l == 2:
                            pe.wait_ge(s_xk[2], b + 1)
                        elif not isinstance(b, int) or b:
                            pe.wait_ge(s_read[l], b)
                    if n in turn_at:
                        r = turn_at[n]
                        if r == 0:
                            pe.wait_ge(s_gather, (run.body_no + 2) * (16 * F) - 16 * N_S)
                        pe.wait_ge(s_x0t, run.body_no * (D // 4) + (D // 4 + r - 1))
                    if not is_split(g):
                        pe.wait_ge(s_prod, run.products(n))
                    complete(run, n) if g.tiles == GROUPS[l][-1] else add(run, n)
                    if n in turn_at:
                        turn(turn_at[n])

            def hidden1(bank, m, c0, n, stop):
                ms = slice(m * P, (m + 1) * P)
                pe.matmul(bank[:, 0:n], wt_dense[:, ms], dense_t[:, c0:c0 + n], start=True, stop=False)
                mm = pe.matmul(bank[:, 0:n], wt1[:, 0, ms], sums[:, 0, c0:c0 + n], start=False, stop=False)
                if stop:
                    mm = pe.matmul(bank[:, 0:n], wt1[:, 1, ms], sums[:, 1, c0:c0 + n], start=False, stop=True)
                return mm

            def hidden2(bank, m, c, n):
                return pe.matmul(bank[:, 0:n], wt2[:, c, m * P:(m + 1) * P], h1[:, c, 0:n],
                                 start=(c == 0), stop=(c == H1 // P - 1))

            def last_layer(bank, n, done):
                for c in range(H2 // P):
                    pe.wait_ge(s_mlp_act, done + H1 // P + c + 1)
                    mm = pe.matmul(bank[0:1, 0:n], wt3[:, c:c + 1], h2[:, c, 0:n],
                                   start=(c == 0), stop=(c == H2 // P - 1))
                mm.then_inc(s_mlp_mm, 1)

            def mlp_main():
                pe.wait_ge(s_mlpw, 16 * N_MLPW)
                pe.wait_ge(s_x0t, BT * (D // 4))
                pe.wait_ge(s_sum2, NB - 1)
                pe.wait_ge(s_sum01, NB - 1)
                for m in range(H1 // P):
                    if m >= 2:
                        pe.wait_ge(s_mlp_act, m - 1)
                    hidden1(MLP_BANKS[m], m, 0, MAIN, True).then_inc(s_mlp_mm, 1)
                for m in range(H2 // P):
                    q = H1 // P + m
                    pe.wait_ge(s_mlp_act, q - 1)
                    for c in range(H1 // P):
                        pe.wait_ge(s_mlp_act, max(c + 1, q - 1))
                        mm = hidden2(MLP_BANKS[q], m, c, MAIN)
                    mm.then_inc(s_mlp_mm, 1)
                pe.wait_ge(s_mlp_act, MLP_STEPS - 2)
                last_layer(MLP_BANKS[-1], MAIN, 0)

            def mlp_ahead():
                pe.wait_ge(s_sum01, NB)
                pe.wait_ge(s_read[0], NB)
                pe.wait_ge(s_read[1], NB)
                for m in range(H1 // P):
                    hidden1(LAST_BANKS[m], m, MAIN, BB, False)

            def mlp_last():
                for c, data in enumerate((sums[:, 1, MAIN:], last_sum[:])):
                    pe.wait_ge(s_sum2, NB + c)
                    for m in range(H1 // P):
                        mm = pe.matmul(LAST_BANKS[m][:, 0:BB], wt1[:, 1, m * P:(m + 1) * P], data,
                                       start=False, stop=bool(c))
                        if c:
                            mm.then_inc(s_mlp_mm, 1)
                for c in range(H1 // P):
                    pe.wait_ge(s_mlp_act, MLP_STEPS + c + 1)
                    for m in range(H2 // P):
                        mm = hidden2(spare[m], m, c, BB)
                        if c == H1 // P - 1:
                            mm.then_inc(s_mlp_mm, 1)
                last_layer(LAST_BANKS[-1], BB, MLP_STEPS)

            groups(Run(prologue), {})
            with nc.Fori(0, BT - 1, engines=[mybir.EngineType.PE], hint_back_edge=True) as bt:
                groups(Run(body, bt), TURN_AT)
            groups(Run(tail, BT - 1), {}, mlp_at=HALF - AHEAD)
            mlp_last()


def kernel(**inputs):
    import numpy as _np
    import concourse.bacc as _bacc
    from concourse import mybir as _mybir
    from concourse.bass_utils import run_bass_kernel_spmd as _run

    nc = _bacc.Bacc("TRN2", target_bir_lowering=False, num_devices=1)
    arrays = {}

    def given(name):
        a = _np.ascontiguousarray(inputs[name])
        arrays[f"in_{name}_dram"] = a
        return nc.dram_tensor(f"in_{name}_dram", a.shape, _mybir.dt.from_np(a.dtype), kind="ExternalInput").ap()

    n_tables = inputs["ids"].shape[1]
    out = nc.dram_tensor("out_0_dram", (inputs["ids"].shape[0], 1), _mybir.dt.float32, kind="ExternalOutput").ap()
    cin_tower(nc, given("dense_ctx"), given("ids"), [given(f"tbl_{i}") for i in range(n_tables)],
              given("W_top1"), given("b_top1"), given("W_top2"), given("b_top2"), given("W_top3"),
              [given(f"L0_rec_w{i}") for i in range(3)], [given(f"L0_rec_b{i}") for i in range(3)], out)
    r = _run(nc, [arrays], core_ids=[0])
    return r.results[0]["out_0_dram"]
```
